# Optimizing a Trainium2 kernel written in Bass

```python
import numpy as np
import jax
import jax.numpy as jnp

def _softmax(x, axis=-1):
    return jax.nn.softmax(x, axis=axis)

def _gelu(x):
    return jax.nn.gelu(x, approximate=True)

def _silu(x):
    return jax.nn.silu(x)

def _sigmoid(x):
    return jax.nn.sigmoid(x)

def _layernorm(x, axis=-1, eps=1e-05):
    m = jnp.mean(x, axis=axis, keepdims=True)
    v = jnp.var(x, axis=axis, keepdims=True)
    return (x - m) / jnp.sqrt(v + eps)

def _scatter_add(tgt, idx, src, axis=0):
    return tgt.at[idx].add(src)

def _segment_sum(src, seg, n):
    return jax.ops.segment_sum(src, seg, n)
kernel_name = 'mk_seq_postln_d1_jaxref_r8_c26a89'

def setup_inputs(seed: int=0):
    np.random.seed(seed)
    _w = jnp.asarray

    def _L0_attn_setup():
        import jax, jax.numpy as jnp
        import numpy as np
        EPS = 1e-06
        CHUNK = 64
        GATE_LOGIT_NORMALIZER = 16.0
        NUM_HEADS = 4

        def _rms(x, w):
            return x * jax.lax.rsqrt(jnp.mean(x * x, axis=-1, keepdims=True) + EPS) * w

        def _gla_chunk(q, k, v, glog, num_heads):
            B, T, Dk = q.shape
            Dv = v.shape[-1]
            dk, dv = (Dk // num_heads, Dv // num_heads)
            Nc = T // CHUNK

            def split(x, d):
                return x.reshape(B, T, num_heads, d).transpose(0, 2, 1, 3).reshape(B, num_heads, Nc, CHUNK, d)
            q, k, v, g = (split(q, dk), split(k, dk), split(v, dv), split(glog, dk))
            b = jnp.cumsum(g, axis=3)
            scale = dk ** (-0.5)
            qe = q * jnp.exp(b) * scale
            mask = jnp.tril(jnp.ones((CHUNK, CHUNK), dtype=bool))
            A = jnp.einsum('bhncd,bhnsd->bhncs', qe, k * jnp.exp(-b))
            A = jnp.where(mask, A, 0.0)
            o_intra = jnp.einsum('bhncs,bhnsd->bhncd', A, v)

            def step(S, xs):
                qe_c, k_c, v_c, b_c = xs
                blast = b_c[:, :, -1, :]
                o_inter = jnp.einsum('bhcd,bhde->bhce', qe_c, S)
                kd = k_c * jnp.exp(blast[:, :, None, :] - b_c)
                S_new = S * jnp.exp(blast)[..., None] + jnp.einsum('bhcd,bhce->bhde', kd, v_c)
                return (S_new, o_inter)
            S0 = jnp.zeros((B, num_heads, dk, dv), q.dtype)
            xs = tuple((jnp.moveaxis(t, 2, 0) for t in (qe, k, v, b)))
            _, o_inter = jax.lax.scan(step, S0, xs)
            o = o_intra + jnp.moveaxis(o_inter, 0, 2)
            return o.reshape(B, num_heads, T, dv).transpose(0, 2, 1, 3)
        key = jax.random.key(seed)
        ks = jax.random.split(key, 12)
        B, T, Hs = (4, 256, 128)
        Dk, Dv, I, R = (64, 128, 352, 16)
        p = lambda k, s: jax.random.normal(k, s, jnp.float32) * 0.02
        return {'hidden_states': jax.random.normal(ks[0], (B, T, Hs), jnp.float32), 'attn_norm_w': jnp.ones((Hs,), jnp.float32), 'Wq': p(ks[1], (Hs, Dk)), 'Wk': p(ks[2], (Hs, Dk)), 'Wv': p(ks[3], (Hs, Dv)), 'Wg': p(ks[4], (Hs, Dv)), 'Wgk1': p(ks[5], (Hs, R)), 'Wgk2': p(ks[6], (R, Dk)), 'bgk2': jnp.zeros((Dk,), jnp.float32), 'gnorm_w': jnp.ones((Dv // NUM_HEADS,), jnp.float32), 'Wo': p(ks[7], (Dv, Hs)), 'mlp_norm_w': jnp.ones((Hs,), jnp.float32), 'W_gate': p(ks[8], (Hs, I)), 'W_up': p(ks[9], (Hs, I)), 'W_down': p(ks[10], (I, Hs))}
    _L0_attn_in = _L0_attn_setup()

    def _L0_ffn_setup():
        import jax, jax.numpy as jnp
        import numpy as np

        def _binarize(w):
            alpha = jax.lax.stop_gradient(jnp.mean(jnp.abs(w), axis=1, keepdims=True))
            bw = alpha * jnp.sign(w)
            return w + jax.lax.stop_gradient(bw - w)
        key = jax.random.key(seed)
        k1, k2, k3, k4, k5 = jax.random.split(key, 5)
        D, H = (128, 512)
        x = jax.random.normal(k1, (64, 196, D), dtype=jnp.float32)
        w1 = jax.random.normal(k2, (H, D), dtype=jnp.float32) * 0.02
        b1 = jax.random.normal(k3, (H,), dtype=jnp.float32) * 0.02
        w2 = jax.random.normal(k4, (D, H), dtype=jnp.float32) * 0.02
        b2 = jax.random.normal(k5, (D,), dtype=jnp.float32) * 0.02
        return {'x': x, 'w1': w1, 'b1': b1, 'w2': w2, 'b2': b2}
    _L0_ffn_in = _L0_ffn_setup()
    _d = {'L0_attn_hidden_states': _L0_attn_in['hidden_states'], 'L0_attn_attn_norm_w': _L0_attn_in['attn_norm_w'], 'L0_attn_Wq': _L0_attn_in['Wq'], 'L0_attn_Wk': _L0_attn_in['Wk'], 'L0_attn_Wv': _L0_attn_in['Wv'], 'L0_attn_Wg': _L0_attn_in['Wg'], 'L0_attn_Wgk1': _L0_attn_in['Wgk1'], 'L0_attn_Wgk2': _L0_attn_in['Wgk2'], 'L0_attn_bgk2': _L0_attn_in['bgk2'], 'L0_attn_gnorm_w': _L0_attn_in['gnorm_w'], 'L0_attn_Wo': _L0_attn_in['Wo'], 'L0_attn_mlp_norm_w': _L0_attn_in['mlp_norm_w'], 'L0_attn_W_gate': _L0_attn_in['W_gate'], 'L0_attn_W_up': _L0_attn_in['W_up'], 'L0_attn_W_down': _L0_attn_in['W_down'], 'L0_ffn_w1': _L0_ffn_in['w1'], 'L0_ffn_b1': _L0_ffn_in['b1'], 'L0_ffn_w2': _L0_ffn_in['w2'], 'L0_ffn_b2': _L0_ffn_in['b2']}
    _x0 = _d['L0_attn_hidden_states']
    _d['L0_attn_hidden_states'] = jax.random.normal(jax.random.fold_in(jax.random.key(seed), 1), (8, 256, 128), dtype=_x0.dtype)
    del _x0
    return _d

def reference(L0_attn_hidden_states, L0_attn_attn_norm_w, L0_attn_Wq, L0_attn_Wk, L0_attn_Wv, L0_attn_Wg, L0_attn_Wgk1, L0_attn_Wgk2, L0_attn_bgk2, L0_attn_gnorm_w, L0_attn_Wo, L0_attn_mlp_norm_w, L0_attn_W_gate, L0_attn_W_up, L0_attn_W_down, L0_ffn_w1, L0_ffn_b1, L0_ffn_w2, L0_ffn_b2):

    def _L0_attn_ref(hidden_states, attn_norm_w, Wq, Wk, Wv, Wg, Wgk1, Wgk2, bgk2, gnorm_w, Wo, mlp_norm_w, W_gate, W_up, W_down):
        import jax, jax.numpy as jnp
        import numpy as np
        EPS = 1e-06
        CHUNK = 64
        GATE_LOGIT_NORMALIZER = 16.0
        NUM_HEADS = 4

        def _rms(x, w):
            return x * jax.lax.rsqrt(jnp.mean(x * x, axis=-1, keepdims=True) + EPS) * w

        def _gla_chunk(q, k, v, glog, num_heads):
            B, T, Dk = q.shape
            Dv = v.shape[-1]
            dk, dv = (Dk // num_heads, Dv // num_heads)
            Nc = T // CHUNK

            def split(x, d):
                return x.reshape(B, T, num_heads, d).transpose(0, 2, 1, 3).reshape(B, num_heads, Nc, CHUNK, d)
            q, k, v, g = (split(q, dk), split(k, dk), split(v, dv), split(glog, dk))
            b = jnp.cumsum(g, axis=3)
            scale = dk ** (-0.5)
            qe = q * jnp.exp(b) * scale
            mask = jnp.tril(jnp.ones((CHUNK, CHUNK), dtype=bool))
            A = jnp.einsum('bhncd,bhnsd->bhncs', qe, k * jnp.exp(-b))
            A = jnp.where(mask, A, 0.0)
            o_intra = jnp.einsum('bhncs,bhnsd->bhncd', A, v)

            def step(S, xs):
                qe_c, k_c, v_c, b_c = xs
                blast = b_c[:, :, -1, :]
                o_inter = jnp.einsum('bhcd,bhde->bhce', qe_c, S)
                kd = k_c * jnp.exp(blast[:, :, None, :] - b_c)
                S_new = S * jnp.exp(blast)[..., None] + jnp.einsum('bhcd,bhce->bhde', kd, v_c)
                return (S_new, o_inter)
            S0 = jnp.zeros((B, num_heads, dk, dv), q.dtype)
            xs = tuple((jnp.moveaxis(t, 2, 0) for t in (qe, k, v, b)))
            _, o_inter = jax.lax.scan(step, S0, xs)
            o = o_intra + jnp.moveaxis(o_inter, 0, 2)
            return o.reshape(B, num_heads, T, dv).transpose(0, 2, 1, 3)
        x = hidden_states
        h = _rms(x, attn_norm_w)
        q, k, v = (h @ Wq, h @ Wk, h @ Wv)
        glog = jax.nn.log_sigmoid(h @ Wgk1 @ Wgk2 + bgk2) / GATE_LOGIT_NORMALIZER
        o = _gla_chunk(q, k, v, glog, NUM_HEADS)
        g_out = (h @ Wg).reshape(o.shape)
        o = _rms(o, gnorm_w) * (g_out * jax.nn.sigmoid(g_out))
        attn_out = o.reshape(x.shape[0], x.shape[1], -1) @ Wo
        x2 = attn_out + x
        n = _rms(x2, mlp_norm_w)
        mlp = jax.nn.silu(n @ W_gate) * (n @ W_up) @ W_down
        return x2 + mlp

    def _L0_ffn_ref(x, w1, b1, w2, b2):
        import jax, jax.numpy as jnp
        import numpy as np

        def _binarize(w):
            alpha = jax.lax.stop_gradient(jnp.mean(jnp.abs(w), axis=1, keepdims=True))
            bw = alpha * jnp.sign(w)
            return w + jax.lax.stop_gradient(bw - w)
        bw1 = _binarize(w1)
        h = jnp.einsum('bsd,hd->bsh', x, bw1) + b1
        h = jax.nn.gelu(h, approximate=False)
        bw2 = _binarize(w2)
        out = jnp.einsum('bsh,dh->bsd', h, bw2) + b2
        return out
    x = L0_attn_hidden_states
    x = _layernorm(x + _L0_attn_ref(x, L0_attn_attn_norm_w, L0_attn_Wq, L0_attn_Wk, L0_attn_Wv, L0_attn_Wg, L0_attn_Wgk1, L0_attn_Wgk2, L0_attn_bgk2, L0_attn_gnorm_w, L0_attn_Wo, L0_attn_mlp_norm_w, L0_attn_W_gate, L0_attn_W_up, L0_attn_W_down), axis=-1)
    x = _layernorm(x + _L0_ffn_ref(x, L0_ffn_w1, L0_ffn_b1, L0_ffn_w2, L0_ffn_b2), axis=-1)
    return x

_drawn_inputs = setup_inputs


def setup_inputs(seed=0):
    import zlib

    import numpy as np

    out = dict(_drawn_inputs(seed))
    spreads = {'L0_attn_attn_norm_w': (1.0, 0.6),
     'L0_attn_bgk2': (0.0, 0.8),
     'L0_attn_gnorm_w': (1.0, 0.6),
     'L0_attn_mlp_norm_w': (1.0, 0.6)}
    factors = {'L0_attn_Wq': 3.973,
     'L0_attn_Wk': 3.96,
     'L0_attn_Wv': 3.943,
     'L0_attn_Wg': 3.988,
     'L0_attn_Wgk1': 8.0,
     'L0_attn_Wgk2': 8.0,
     'L0_attn_Wo': 3.936,
     'L0_attn_W_gate': 8.0,
     'L0_attn_W_up': 8.0,
     'L0_attn_W_down': 8.0,
     'L0_ffn_b1': 8.0,
     'L0_ffn_b2': 2.785}
    for name, (base, spread) in spreads.items():
        noise = np.random.default_rng([zlib.crc32(name.encode()), seed]).standard_normal(out[name].shape)
        drawn = base * np.exp(spread * noise) if base else spread * noise
        out[name] = jnp.asarray(drawn.astype(out[name].dtype))
    for name, factor in factors.items():
        out[name] = (out[name] * factor).astype(out[name].dtype)
    return out
```

```python
from contextlib import ExitStack

import concourse.bass as bass
from concourse import mybir

F32 = mybir.dt.float32
F32R = mybir.dt.float32r
U32 = mybir.dt.uint32
ALU = mybir.AluOpType
ACT = mybir.ActivationFunctionType
AX = mybir.AxisListType

P = 128
RMS_EPS = 1e-6
LN_EPS = 1e-5
GATE_NORMALIZER = 16.0
BATCH_TILES = 2
CHUNK_TILES = 4


def gla_block_and_binary_ffn(nc, x, attn_norm_w, Wq, Wk, Wv, Wg, Wgk1, Wgk2, bgk2, gnorm_w, Wo,
                             mlp_norm_w, W_gate, W_up, W_down, w1, b1, w2, b2, out):
    B, T, D = x.shape
    DK = Wq.shape[1]
    DV = Wv.shape[1]
    R = Wgk1.shape[1]
    E = gnorm_w.shape[0]
    H = DV // E
    HD = DK // H
    HP = P // H
    I = W_gate.shape[1]
    HF = w1.shape[0]
    NB, TB, TC = B, BATCH_TILES, CHUNK_TILES
    NT = B * T // P
    NC = NT // TC
    CH = TC * P
    BT = TB * P
    NI = -(-I // P)
    NF = HF // P
    IW = [min(P, I - j * P) for j in range(NI)]
    QKZ, VG = 2 * DK + DK, 2 * DV
    assert T == BT and D == P and DV == P and H * HP == P and HD <= HP and E == HP
    assert TB * QKZ <= 512 and TB * VG <= 512 and TB * H * P <= 1024 and CH == 512

    with ExitStack() as ctx:
        def sb(name, shape, dt=F32):
            return ctx.enter_context(nc.sbuf_tensor(name, shape, dt))

        def bank(name):
            return ctx.enter_context(nc.psum_tensor(name, [P, 512], F32))

        def sem(name):
            return ctx.enter_context(nc.semaphore(name))

        bank_qkz, bank_vg, bank_turn = bank("bank_qkz"), bank("bank_vg"), bank("bank_turn")
        bank_a = [bank("bank_a0"), bank("bank_a1")]
        bank_o, bank_dx, bank_uw = bank("bank_o"), bank("bank_dx"), bank("bank_uw")
        qkz_ps = bank_qkz[:, 0:TB * QKZ].rearrange("p (t n) -> p t n", t=TB)
        vg_ps = bank_vg[:, :].rearrange("p (t n) -> p t n", t=TB)
        o_ps = bank_o[:, 0:TB * DV].rearrange("p (t n) -> p t n", t=TB)
        xT_ps = bank_dx[:, 0:BT]
        decay_ps = bank_dx[:, BT:BT + TB * DK]
        carry_ps = bank_dx[:, BT + TB * DK:BT + TB * DK + 2]
        kv_ps = bank_uw[:, 0:DV]
        wo_ps = bank_uw[:, DV:DV + TB * D].rearrange("p (t n) -> p t n", t=TB)
        gate_ps = [bank_vg, bank_turn]
        up_ps = bank_a
        down_ps = bank_qkz
        yT_ps = bank_dx
        hid_ps = [bank_o, bank_vg, bank_turn]
        ffn_ps = [bank_uw, bank_qkz]

        ident = sb("ident", [P, P])
        causal = sb("causal", [P, H * P])
        decay_sum = sb("decay_sum", [P, P])
        late_half = sb("late_half", [P, 2])
        early_half = sb("early_half", [P, 2])
        same_head = sb("same_head", [P, DV])
        eps = sb("eps", [P, 1])
        minus_half = sb("minus_half", [P, TC])
        w_in = sb("w_in", [P, 2 * DK + 2 * DV])
        anw = sb("anw", [P, 1])
        gk1_in = sb("gk1_in", [P, R])
        gk2_in = sb("gk2_in", [R, DK])
        z_bias = sb("z_bias", [P, DK])
        wo_in = sb("wo_in", [P, D])
        gnw = sb("gnw", [P, 1])
        mnw = sb("mnw", [P, 1])
        gu_in = sb("gu_in", [P, 2 * I])
        w1_in = sb("w1_in", [P, NF, D])
        w2_in = sb("w2_in", [P, HF])
        b1_col = sb("b1_col", [P, NF])
        b2_row = sb("b2_row", [P, D])
        gk1T = sb("gk1T", [R, P])
        w_qkz = sb("w_qkz", [P, QKZ])
        w_vg = sb("w_vg", [P, VG])
        w_o = sb("w_o", [P, D])
        w_gu = sb("w_gu", [P, 2 * I])
        w_down = sb("w_down", [P, NI, D])
        neg1 = sb("neg1", [P, NF, D])
        sign1 = sb("sign1", [P, NF, D])
        neg2 = sb("neg2", [P, HF])
        sign2 = sb("sign2", [P, HF])
        bin2 = sb("bin2", [P, HF])
        abs1 = sb("abs1", [P, NF])
        alpha1 = sb("alpha1", [P, NF])
        abs2 = sb("abs2", [P, 1])
        alpha2 = sb("alpha2", [P, 1])
        sign1T = sb("sign1T", [P, HF], F32R)
        bin2T = sb("bin2T", [P, NF, D])
        xs = sb("xs", [P, NT, D])
        x_ssq = sb("x_ssq", [P, NT])
        x_ln = sb("x_ln", [P, NT])
        x_rs = sb("x_rs", [P, NT])
        xh = sb("xh", [P, NT, D])
        xT = sb("xT", [P, NT * P])
        zb = sb("zb", [P, TB, DK])
        z_na = sb("z_na", [P, TB, DK])
        z_e = sb("z_e", [P, TB, DK])
        z_l = sb("z_l", [P, TB, DK])
        glog = sb("glog", [P, 2, TB, P])
        vg = sb("vg", [P, NT, VG])
        g_na = sb("g_na", [P, TB, DV])
        g_e = sb("g_e", [P, TB, DV])
        g_l = sb("g_l", [P, TB, DV])
        g_ls = sb("g_ls", [P, TB, DV])
        g_sg = sb("g_sg", [P, TB, DV])
        gs = sb("gs", [P, 2, TB, DV])
        grow = sb("grow", [P, TB * DK])
        fall = sb("fall", [P, TB * DK])
        carry = sb("carry", [P, 2, 2])
        qe = sb("qe", [P, 2, TB, P])
        ke = sb("ke", [P, 2, TB, P])
        kT = sb("kT", [P, 2, BT])
        qT1 = sb("qT1", [P, 2, P])
        qheads = sb("qheads", [P, 2, TB, H, P])
        att = sb("att", [P, 2, TB, H * P])
        state = sb("state", [P, 2, DV])
        o_sb = sb("o_sb", [P, 2, TB, DV])
        o_sq = sb("o_sq", [P, 2, TB, DV])
        o_ssq = sb("o_ssq", [P, NT, H])
        o_ln = sb("o_ln", [P, NT, H])
        o_rs = sb("o_rs", [P, NT, H])
        o_n = sb("o_n", [P, TB, DV])
        og = sb("og", [P, 2, TB, DV])
        onT = sb("onT", [P, NB + 1, 2, BT])
        x2 = sb("x2", [P, NT, D])
        x2_ssq = sb("x2_ssq", [P, NT])
        x2_ln = sb("x2_ln", [P, NT])
        x2_rs = sb("x2_rs", [P, NT])
        n_sb = sb("n_sb", [P, 2, TB, D])
        xx2 = sb("xx2", [P, NT, D])
        gate_s = sb("gate_s", [P, 2, CH])
        act_T = sb("act_T", [P, 3, CH])
        ln_in = sb("ln_in", [P, 2, TC, D])
        ln_st = sb("ln_st", [P, 2, TC, 6])
        ln_mv = sb("ln_mv", [P, 2, TC, 2])
        ln_ve = sb("ln_ve", [P, 2, TC])
        ln_rs = sb("ln_rs", [P, 2, TC])
        y = sb("y", [P, NT, D])
        yb = sb("yb", [P, NT, D])
        y_hi = sb("y_hi", [P, 2, CH], F32R)
        y_lo = sb("y_lo", [P, 2, CH], F32R)
        hid = sb("hid", [P, 3, CH])
        y_out = sb("y_out", [P, NT, D])

        x_in = [sem(f"x_in{b}") for b in range(NB)]
        attn_w_in, gk_in, wo_w_in, mlp_w_in = sem("attn_w_in"), sem("gk_in"), sem("wo_w_in"), sem("mlp_w_in")
        down_w_in, ffn_w_in, out_done = sem("down_w_in"), sem("ffn_w_in"), sem("out_done")
        names = """eps_ok ident_ok consts_zero up_to_ok same_zero consts_ok pads_ok gk1T_ps gk1T_ok gkw_ps w_attn_ok w_o_ok w_gu_ok
            half1_ok sign1_ok half2_ok sign2_ok abs_ok alpha_ok bin2_ok sign1T_ps sign1T_ok bin2T_ps bin2T_ok
            xssq_ok xln_ok xrs_ok xh_ok xT_pe xT_ok qkz_pe vg_pe vg_ok zb_ok zna_ok ze_ok zl_ok glog_ok
            gna_ok ge_ok gl_ok gls_ok gsg_ok gs_ok carry_pe grow_ok fall_ok carry_ok qe_ok ke_ok
            turn_pe kT_ok qheads_ok a_pe att_ok kv_pe kv_ok o_pe o_ok osq_ok ossq_ok oln_ok ors_ok
            on_ok og_ok ogT_pe onT_ok wo_pe x2_ok x2ssq_ok x2ln_ok x2rs_ok n_ok xx2_ok
            gate_pe up_pe gates_ok act_ok down_pe t1_ok st1_ok mv1_ok ve1_ok rs1_ok y_ok yb_ok
            yT_pe yhi_ok ylo_ok hid_pe hid_ok ffn_pe t2_ok st2_ok mv2_ok ve2_ok rs2_ok yout_ok""".split()
        S = {n: sem(n) for n in names}

        def tiles(b):
            return slice(b * TB, (b + 1) * TB)

        def ctiles(c):
            return slice(c * TC, (c + 1) * TC)

        block = ctx.enter_context(nc.Block())

        @block.sync
        def _(sp):
            xv = x.rearrange("b (t p) d -> p (b t) d", p=P)
            ov = out.rearrange("b (t p) d -> p (b t) d", p=P)
            sp.dma_start(xs[:, tiles(0), :], xv[:, tiles(0), :]).then_inc(x_in[0], 16)
            sp.dma_start(w_in[:, 0:DK], Wq).then_inc(attn_w_in, 16)
            sp.dma_start(w_in[:, DK:2 * DK], Wk).then_inc(attn_w_in, 16)
            sp.dma_start(xs[:, tiles(1), :], xv[:, tiles(1), :]).then_inc(x_in[1], 16)
            sp.dma_start(xs[:, tiles(2), :], xv[:, tiles(2), :]).then_inc(x_in[2], 16)
            sp.dma_start(wo_in[:, :], Wo).then_inc(wo_w_in, 16)
            for h in range(H):
                sp.dma_start(gnw[h * E:(h + 1) * E, :], gnorm_w.rearrange("(e a) -> e a", a=1)).then_inc(wo_w_in, 16)
            for b in range(3, NB):
                sp.dma_start(xs[:, tiles(b), :], xv[:, tiles(b), :]).then_inc(x_in[b], 16)
            sp.dma_start(gu_in[:, 0:I], W_gate).then_inc(mlp_w_in, 16)
            sp.dma_start(gu_in[:, I:2 * I], W_up).then_inc(mlp_w_in, 16)
            sp.dma_start(mnw[:, :], mlp_norm_w.rearrange("(p a) -> p a", a=1)).then_inc(mlp_w_in, 16)
            sp.dma_start(w1_in[:, :, :], w1.rearrange("(p j) d -> p j d", p=P)).then_inc(ffn_w_in, 16)
            sp.dma_start(w2_in[:, :], w2).then_inc(ffn_w_in, 16)
            sp.dma_start(b1_col[:, :], b1.rearrange("(p j) -> p j", p=P)).then_inc(ffn_w_in, 16)
            sp.dma_start(b2_row[:, :], b2.partition_broadcast(P)).then_inc(ffn_w_in, 16)
            for j in range(NI):
                sp.dma_start(w_down[0:IW[j], j, :], W_down[j * P:j * P + IW[j], :]).then_inc(down_w_in, 16)
            for c in range(NC):
                sp.wait_ge(S["yout_ok"], c + 1)
                sp.dma_start(ov[:, ctiles(c), :], y_out[:, ctiles(c), :]).then_inc(out_done, 16)
            sp.wait_ge(out_done, 16 * NC)

        @block.gpsimd
        def _(pool):
            pool.memset(ident[:, :], 0.0)
            pool.memset(decay_sum[:, :], 0.0)
            pool.memset(causal[:, :], 0.0).then_inc(S["consts_zero"], 1)
            pool.wait_ge(S["consts_zero"], 1)
            pool.affine_select(out=ident[:, :], in_=ident[:, :], compare_op=ALU.not_equal, fill=1.0, base=0,
                               pattern=[[-1, P]], channel_multiplier=1).then_inc(S["ident_ok"], 1)
            pool.affine_select(out=decay_sum[:, :], in_=decay_sum[:, :], compare_op=ALU.is_gt,
                               fill=1.0 / GATE_NORMALIZER, base=0, pattern=[[-1, P]], channel_multiplier=1)\
                .then_inc(S["up_to_ok"], 1)
            pool.memset(glog[:, :, :, :], 0.0)
            pool.memset(qe[:, :, :, :], 0.0)
            pool.memset(ke[:, :, :, :], 0.0)
            pool.memset(qheads[:, :, :, :, :], 0.0).then_inc(S["pads_ok"], 1)
            pool.affine_select(out=causal[:, :], in_=causal[:, :], compare_op=ALU.is_gt, fill=1.0, base=0,
                               pattern=[[0, H], [-1, P]], channel_multiplier=1)
            pool.memset(att[:, :, :, :], 0.0).then_inc(S["pads_ok"], 1)
            pool.memset(minus_half[:, :], -0.5)

            def gate_product(b):
                pool.wait_ge(S["gsg_ok"], b + 1)
                pool.wait_ge(S["vg_ok"], b + 1)
                if b >= 2:
                    pool.wait_ge(S["og_ok"], b - 1)
                pool.tensor_tensor(gs[:, b % 2], vg[:, tiles(b), DV:VG], g_sg[:, :, :], ALU.mult).then_inc(S["gs_ok"], 1)

            def o_squares(b):
                pool.wait_ge(S["o_ok"], b + 1)
                if b >= 2:
                    pool.wait_ge(S["ossq_ok"], b - 1)
                pool.tensor_tensor(o_sq[:, b % 2], o_sb[:, b % 2], o_sb[:, b % 2], ALU.mult).then_inc(S["osq_ok"], 1)

            def x_plus_x2(b):
                pool.wait_ge(S["x2_ok"], b + 1)
                pool.tensor_tensor(xx2[:, tiles(b), :], xs[:, tiles(b), :], x2[:, tiles(b), :], ALU.add)\
                    .then_inc(S["xx2_ok"], 1)

            for k in range(-1, NB + 1):
                if 0 <= k + 1 < NB:
                    gate_product(k + 1)
                if 0 <= k < NB:
                    o_squares(k)
                if 0 <= k - 1 < NB:
                    x_plus_x2(k - 1)

            def root(which, c):
                pool.wait_ge(S["mv" + which], c + 1)
                if c >= 2:
                    pool.wait_ge(S[("y_ok" if which == "1_ok" else "yout_ok")], c - 1)
                pool.tensor_scalar(ln_ve[:, c % 2], ln_mv[:, c % 2, :, 1], LN_EPS, 1.0, ALU.add, ALU.mult)\
                    .then_inc(S["ve" + which], 1)
                pool.wait_ge(S["ve" + which], c + 1)
                pool.tensor_tensor(ln_rs[:, c % 2], ln_ve[:, c % 2], minus_half[:, :], ALU.pow)\
                    .then_inc(S["rs" + which], 1)

            pool.wait_ge(ffn_w_in, 64)
            for c in range(NC):
                root("1_ok", c)
                pool.wait_ge(S["y_ok"], c + 1)
                for t in range(TC):
                    i = c * TC + t
                    ins = pool.tensor_tensor(yb[:, i, :], y[:, i, :], b2_row[:, :], ALU.add)
                ins.then_inc(S["yb_ok"], 1)
            for c in range(NC):
                root("2_ok", c)

        @block.tensor
        def _(pe):
            def turn_x(b):
                pe.wait_ge(S["xh_ok"], b + 1)
                if b >= 1:
                    pe.wait_ge(S["xT_ok"], b)
                if b >= 2:
                    pe.wait_ge(S["carry_ok"], b - 1)
                for t in range(TB):
                    ins = pe.transpose(xT_ps[:, t * P:(t + 1) * P], xh[:, b * TB + t, :], ident[:, :])
                ins.then_inc(S["xT_pe"], 1)

            def project(b):
                if b == 0:
                    pe.wait_ge(S["w_attn_ok"], 3)
                pe.wait_ge(S["xT_ok"], b + 1)
                if b >= 1:
                    pe.wait_ge(S["ke_ok"], b)
                for t in range(TB):
                    i = b * TB + t
                    ins = pe.matmul(qkz_ps[:, t, :], xT[:, i * P:(i + 1) * P], w_qkz[:, :], start=True, stop=True)
                ins.then_inc(S["qkz_pe"], 1)
                if b >= 1:
                    pe.wait_ge(S["vg_ok"], b)
                if b >= 3:
                    pe.wait_ge(S["onT_ok"], b - 2)
                for t in range(TB):
                    i = b * TB + t
                    ins = pe.matmul(vg_ps[:, t, :], xT[:, i * P:(i + 1) * P], w_vg[:, :], start=True, stop=True)
                ins.then_inc(S["vg_pe"], 1)

            def decay(b):
                pe.wait_ge(S["glog_ok"], b + 1)
                if b >= 1:
                    pe.wait_ge(S["carry_ok"], b)
                pe.wait_ge(S["xT_ok"], min(b + 2, NB))
                g4 = glog[:, b % 2].rearrange("p t (h d) -> p (t h) d", d=HP)[:, :, 0:HD]
                pe.matmul(decay_ps, decay_sum[:, :], g4, start=True, stop=True)
                pe.matmul(carry_ps, glog[:, b % 2, 0, :], late_half[:, :], start=True, stop=False)
                pe.matmul(carry_ps, glog[:, b % 2, 1, :], early_half[:, :], start=False, stop=True)\
                    .then_inc(S["carry_pe"], 1)

            def turn_qk(b):
                pe.wait_ge(S["qe_ok"], b + 1)
                pe.wait_ge(S["ke_ok"], b + 1)
                if b >= 1:
                    pe.wait_ge(S["qheads_ok"], b)
                for t in range(TB):
                    pe.transpose(bank_turn[:, t * P:(t + 1) * P], ke[:, b % 2, t, :], ident[:, :])
                for t in range(TB):
                    ins = pe.transpose(bank_turn[:, BT + t * P:BT + (t + 1) * P], qe[:, b % 2, t, :], ident[:, :])
                ins.then_inc(S["turn_pe"], 1)

            def scores(b):
                pe.wait_ge(S["kT_ok"], b + 1)
                pe.wait_ge(S["qheads_ok"], b + 1)
                for t in range(TB):
                    if b >= 1:
                        pe.wait_ge(S["att_ok"], TB * (b - 1) + t + 1)
                    pe.matmul(bank_a[t][:, :], kT[:, b % 2, t * P:(t + 1) * P],
                              qheads[:, b % 2, t].rearrange("p h c -> p (h c)"),
                              start=True, stop=True).then_inc(S["a_pe"], 1)

            def key_values(b):
                if b >= 2:
                    pe.wait_ge(S["x2_ok"], b - 1)
                pe.matmul(kv_ps, ke[:, b % 2, 0, :], vg[:, b * TB, 0:DV], start=True, stop=True)\
                    .then_inc(S["kv_pe"], 1)

            def outputs(b, t):
                pe.wait_ge(S["att_ok"], TB * b + t + 1)
                if t == 0 and b >= 1:
                    pe.wait_ge(S["o_ok"], b)
                for h in range(H):
                    pe.matmul(o_ps[:, t, h * E:(h + 1) * E], att[:, b % 2, t, h * P:(h + 1) * P],
                              vg[:, b * TB + t, h * E:(h + 1) * E], start=(t == 0 and h == 0), stop=False,
                              skip_group_check=True)
                if t == 1:
                    pe.wait_ge(S["kv_ok"], b + 1)
                    pe.matmul(o_ps[:, 1, :], qT1[:, b % 2, :], state[:, b % 2, :], start=False, stop=True,
                              skip_group_check=True).then_inc(S["o_pe"], 1)

            def turn_og_n(s):
                if s < NB:
                    pe.wait_ge(S["og_ok"], s + 1)
                if s >= 1:
                    pe.wait_ge(S["n_ok"], s)
                    pe.wait_ge(S["onT_ok"], s)
                pe.wait_ge(S["vg_ok"], min(s + 2, NB))
                for t in range(TB):
                    if s < NB:
                        ins = pe.transpose(bank_vg[:, t * P:(t + 1) * P], og[:, s % 2, t, :], ident[:, :])
                for t in range(TB):
                    if s >= 1:
                        ins = pe.transpose(bank_vg[:, BT + t * P:BT + (t + 1) * P], n_sb[:, (s - 1) % 2, t, :],
                                           ident[:, :])
                ins.then_inc(S["ogT_pe"], 1)

            def project_out(b):
                if b == 0:
                    pe.wait_ge(S["w_o_ok"], 1)
                pe.wait_ge(S["onT_ok"], b + 1)
                pe.wait_ge(S["kv_ok"], min(b + 2, NB))
                if b >= 1:
                    pe.wait_ge(S["x2_ok"], b)
                for t in range(TB):
                    ins = pe.matmul(wo_ps[:, t, :], onT[:, b, 0, t * P:(t + 1) * P], w_o[:, :], start=True, stop=True)
                ins.then_inc(S["wo_pe"], 1)

            pe.wait_ge(S["ident_ok"], 1)
            pe.wait_ge(gk_in, 48)
            pe.transpose(bank_uw[0:R, 0:P], gk1_in[:, :], ident[:, :]).then_inc(S["gk1T_ps"], 1)
            pe.wait_ge(S["gk1T_ok"], 1)
            pe.matmul(bank_uw[:, 0:DK], gk1T[:, :], gk2_in[:, :], start=True, stop=True).then_inc(S["gkw_ps"], 1)
            pe.wait_ge(S["consts_ok"], 1)

            for k in range(-3, NB + 2):
                if 0 <= k < NB:
                    scores(k)
                    key_values(k)
                    outputs(k, 0)
                if 0 <= k + 1 < NB:
                    decay(k + 1)
                if 0 <= k < NB:
                    outputs(k, 1)
                if 0 <= k - 1 <= NB:
                    turn_og_n(k - 1)
                if 0 <= k + 1 < NB:
                    turn_qk(k + 1)
                if 0 <= k + 3 < NB:
                    turn_x(k + 3)
                if 0 <= k - 1 < NB:
                    project_out(k - 1)
                if 0 <= k + 2 < NB:
                    project(k + 2)
                if k == NB:
                    pe.wait_ge(S["sign1_ok"], 1)
                    pe.wait_ge(S["xT_ok"], NB)
                    pe.wait_ge(S["carry_ok"], NB)
                    for j in range(NF):
                        ins = pe.transpose(bank_dx[:, j * P:(j + 1) * P], sign1[:, j, :], ident[:, :])
                    ins.then_inc(S["sign1T_ps"], 1)
                    pe.wait_ge(S["bin2_ok"], 1)
                    pe.wait_ge(S["o_ok"], NB)
                    for j in range(NF):
                        ins = pe.transpose(bank_o[:, j * P:(j + 1) * P], bin2[:, j:HF:NF], ident[:, :])
                    ins.then_inc(S["bin2T_ps"], 1)

            def gate_up(n):
                c, j = divmod(n, NI)
                nT = onT[:, 2 * c + 1:2 * c + 3, 1, :]
                if n == 0:
                    pe.wait_ge(S["w_gu_ok"], 1)
                    pe.wait_ge(S["onT_ok"], NB + 1)
                if n >= 2:
                    pe.wait_ge(S["gates_ok"], n - 1)
                pe.matmul(gate_ps[n % 2][0:IW[j], :], w_gu[:, j * P:j * P + IW[j]], nT, start=True, stop=True)\
                    .then_inc(S["gate_pe"], 1)
                if n >= 2:
                    pe.wait_ge(S["act_ok"], n - 1)
                pe.matmul(up_ps[n % 2][0:IW[j], :], w_gu[:, I + j * P:I + j * P + IW[j]], nT, start=True, stop=True)\
                    .then_inc(S["up_pe"], 1)

            def down(n):
                c, j = divmod(n, NI)
                pe.wait_ge(S["act_ok"], n + 1)
                if n == 0:
                    pe.wait_ge(down_w_in, 16 * NI)
                if j == 0 and c >= 1:
                    pe.wait_ge(S["t1_ok"], c)
                for t in range(TC):
                    ins = pe.matmul(down_ps[:, t * P:(t + 1) * P], act_T[0:IW[j], n % 3, t * P:(t + 1) * P],
                                    w_down[0:IW[j], j, :], start=(j == 0 and t == 0), stop=(j == NI - 1),
                                    skip_group_check=True)
                ins.then_inc(S["down_pe"], 1)

            for n in range(NC * NI):
                gate_up(n)
                if n >= 1:
                    down(n - 1)
            def turn_y(c):
                pe.wait_ge(S["y_ok"], c + 1)
                if c >= 1:
                    pe.wait_ge(S["ylo_ok"], c)
                if c == 0:
                    pe.wait_ge(S["sign1T_ok"], 1)
                for t in range(TC):
                    ins = pe.transpose(yT_ps[:, t * P:(t + 1) * P], y[:, c * TC + t, :], ident[:, :])
                ins.then_inc(S["yT_pe"], 1)

            def hidden(n):
                c, j = divmod(n, NF)
                if n >= 3:
                    pe.wait_ge(S["hid_ok"], n - 2)
                pe.wait_ge(S["yhi_ok"], c + 1)
                if n == 0:
                    pe.wait_ge(S["bin2T_ok"], 1)
                    pe.wait_ge(S["gates_ok"], NC * NI)
                w = sign1T[:, j * P:(j + 1) * P]
                pe.matmul(hid_ps[n % 3][:, :], w, y_hi[:, c % 2, :], start=True, stop=False)
                pe.wait_ge(S["ylo_ok"], c + 1)
                pe.matmul(hid_ps[n % 3][:, :], w, y_lo[:, c % 2, :], start=False, stop=True).then_inc(S["hid_pe"], 1)

            def ffn_out(n):
                c, j = divmod(n, NF)
                pe.wait_ge(S["hid_ok"], n + 1)
                if j == 0 and c >= 2:
                    pe.wait_ge(S["t2_ok"], c - 1)
                if n == NF:
                    pe.wait_ge(S["t1_ok"], NC)
                for t in range(TC):
                    ins = pe.matmul(ffn_ps[c % 2][:, t * P:(t + 1) * P], hid[:, n % 3, t * P:(t + 1) * P],
                                    bin2T[:, j, :], start=(j == 0 and t == 0), stop=(j == NF - 1),
                                    skip_group_check=True)
                ins.then_inc(S["ffn_pe"], 1)

            turn_y(0)
            down(NC * NI - 1)
            for n in range(NC * NF):
                hidden(n)
                if n % NF == 1 and n // NF + 1 < NC:
                    turn_y(n // NF + 1)
                if n >= 1:
                    ffn_out(n - 1)
            ffn_out(NC * NF - 1)

        @block.scalar
        def _(act):
            act.dma_start(w_in[:, 2 * DK:2 * DK + DV], Wv).then_inc(attn_w_in, 16)
            act.dma_start(w_in[:, 2 * DK + DV:2 * DK + VG], Wg).then_inc(attn_w_in, 16)
            act.dma_start(anw[:, :], attn_norm_w.rearrange("(p a) -> p a", a=1)).then_inc(attn_w_in, 16)
            act.dma_start(gk1_in[:, :], Wgk1).then_inc(gk_in, 16)
            act.dma_start(gk2_in[:, :], Wgk2).then_inc(gk_in, 16)
            act.dma_start(z_bias[:, :], bgk2.partition_broadcast(P)).then_inc(gk_in, 16)
            nc.scalar.preload_act_table_set("natural_log_exp_and_others")

            def root(ssq_sem, ln_sem, rs_sem, value, ssq, ln, rs, width):
                act.wait_ge(S[ssq_sem], value)
                act.activation(ln, ssq, ACT.Ln, bias=eps[:, :], scale=1.0 / width).then_inc(S[ln_sem], 1)
                act.wait_ge(S[ln_sem], value)
                act.activation(rs, ln, ACT.Exp, scale=-0.5).then_inc(S[rs_sem], 1)

            def root_x(b):
                root("xssq_ok", "xln_ok", "xrs_ok", b + 1, x_ssq[:, tiles(b)], x_ln[:, tiles(b)],
                     x_rs[:, tiles(b)], D)

            def copy_xT(b):
                act.wait_ge(S["xT_pe"], b + 1)
                act.activation(xT[:, b * BT:(b + 1) * BT], xT_ps, ACT.Copy).then_inc(S["xT_ok"], 1)

            def copy_vg(b):
                act.wait_ge(S["vg_pe"], b + 1)
                act.activation(vg[:, tiles(b), :], vg_ps, ACT.Copy).then_inc(S["vg_ok"], 1)

            def soft_z(b):
                act.wait_ge(S["zna_ok"], b + 1)
                if b >= 1:
                    act.wait_ge(S["zl_ok"], b)
                act.activation(z_e[:, :, :], z_na[:, :, :], ACT.Exp).then_inc(S["ze_ok"], 1)
                act.wait_ge(S["ze_ok"], b + 1)
                if b >= 1:
                    act.wait_ge(S["glog_ok"], b)
                act.activation(z_l[:, :, :], z_e[:, :, :], ACT.Ln, bias=1.0).then_inc(S["zl_ok"], 1)

            def soft_g(b):
                act.wait_ge(S["gna_ok"], b + 1)
                act.activation(g_e[:, :, :], g_na[:, :, :], ACT.Exp).then_inc(S["ge_ok"], 1)
                act.wait_ge(S["ge_ok"], b + 1)
                if b >= 1:
                    act.wait_ge(S["gls_ok"], b)
                act.activation(g_l[:, :, :], g_e[:, :, :], ACT.Ln, bias=1.0).then_inc(S["gl_ok"], 1)

            def sigmoid_g(b):
                act.wait_ge(S["gls_ok"], b + 1)
                if b >= 1:
                    act.wait_ge(S["gs_ok"], b)
                act.activation(g_sg[:, :, :], g_ls[:, :, :], ACT.Exp).then_inc(S["gsg_ok"], 1)

            def decays(b):
                act.wait_ge(S["carry_pe"], b + 1)
                if b >= 1:
                    act.wait_ge(S["qe_ok"], b)
                act.activation(grow[:, :], decay_ps, ACT.Exp).then_inc(S["grow_ok"], 1)
                if b >= 1:
                    act.wait_ge(S["ke_ok"], b)
                act.activation(fall[:, :], decay_ps, ACT.Exp, scale=-1.0).then_inc(S["fall_ok"], 1)
                if b >= 2:
                    act.wait_ge(S["kv_ok"], b - 1)
                act.activation(carry[:, b % 2, :], carry_ps, ACT.Exp).then_inc(S["carry_ok"], 1)

            def copy_qk(b):
                act.wait_ge(S["turn_pe"], b + 1)
                if b == 0:
                    act.wait_ge(S["pads_ok"], 1)
                if b >= 2:
                    act.wait_ge(S["a_pe"], TB * (b - 1))
                    act.wait_ge(S["o_pe"], b - 1)
                act.activation(kT[:, b % 2, :], bank_turn[:, 0:BT], ACT.Copy).then_inc(S["kT_ok"], 1)
                act.activation(qT1[:, b % 2, :], bank_turn[:, BT + P:2 * BT], ACT.Copy)
                for h in range(H):
                    rows = slice(h * HP, (h + 1) * HP)
                    ins = act.activation(qheads[rows, b % 2, :, h, :],
                                         bank_turn[rows, BT:2 * BT].rearrange("p (t c) -> p t c", t=TB), ACT.Copy)
                ins.then_inc(S["qheads_ok"], 1)

            def copy_o(b):
                act.wait_ge(S["o_pe"], b + 1)
                if b >= 2:
                    act.wait_ge(S["on_ok"], b - 1)
                    act.wait_ge(S["osq_ok"], b - 1)
                act.activation(o_sb[:, b % 2], o_ps, ACT.Copy).then_inc(S["o_ok"], 1)

            def root_o(b):
                root("ossq_ok", "oln_ok", "ors_ok", b + 1, o_ssq[:, tiles(b), :], o_ln[:, tiles(b), :],
                     o_rs[:, tiles(b), :], E)

            def copy_on(s):
                act.wait_ge(S["ogT_pe"], s + 1)
                a, z = (0 if s < NB else 1), (2 if s >= 1 else 1)
                act.activation(onT[:, s, a:z, :], bank_vg[:, a * BT:z * BT].rearrange("p (a c) -> p a c", c=BT),
                               ACT.Copy).then_inc(S["onT_ok"], 1)

            def root_x2(b):
                root("x2ssq_ok", "x2ln_ok", "x2rs_ok", b + 1, x2_ssq[:, tiles(b)], x2_ln[:, tiles(b)],
                     x2_rs[:, tiles(b)], D)

            act.wait_ge(S["eps_ok"], 1)
            for k in range(-4, NB + 2):
                if 0 <= k + 1 < NB:
                    copy_vg(k + 1)
                    soft_z(k + 1)
                if 0 <= k + 4 < NB:
                    root_x(k + 4)
                if 0 <= k + 1 < NB:
                    soft_g(k + 1)
                if 0 <= k - 2 < NB - 1:
                    root_x2(k - 2)
                if 0 <= k + 1 < NB:
                    decays(k + 1)
                    sigmoid_g(k + 1)
                if 0 <= k < NB:
                    copy_o(k)
                if 0 <= k - 1 <= NB:
                    copy_on(k - 1)
                if 0 <= k + 1 < NB:
                    copy_qk(k + 1)
                if 0 <= k + 3 < NB:
                    copy_xT(k + 3)
                if 0 <= k < NB:
                    root_o(k)
                if k == NB:
                    root_x2(NB - 1)
                    act.wait_ge(S["sign1T_ps"], 1)
                    act.activation(sign1T[:, :], bank_dx[:, :], ACT.Copy).then_inc(S["sign1T_ok"], 1)
                    act.wait_ge(S["bin2T_ps"], 1)
                    act.activation(bin2T[:, :, :], bank_o[:, :].rearrange("p (j d) -> p j d", j=NF), ACT.Copy)\
                        .then_inc(S["bin2T_ok"], 1)

            for n in range(NC * NI):
                j = n % NI
                act.wait_ge(S["gate_pe"], n + 1)
                if n >= 2:
                    act.wait_ge(S["act_ok"], n - 1)
                act.activation(gate_s[0:IW[j], n % 2, :], gate_ps[n % 2][0:IW[j], :], ACT.Silu)\
                    .then_inc(S["gates_ok"], 1)

            def high_y(c):
                act.wait_ge(S["yT_pe"], c + 1)
                if c >= 2:
                    act.wait_ge(S["hid_pe"], NF * (c - 1))
                act.activation(y_hi[:, c % 2, :], yT_ps[:, :], ACT.Copy).then_inc(S["yhi_ok"], 1)

            act.wait_ge(S["alpha_ok"], 2)
            high_y(0)
            for n in range(NC * NF):
                c, j = divmod(n, NF)
                if j == 2 and c + 1 < NC:
                    high_y(c + 1)
                act.wait_ge(S["hid_pe"], n + 1)
                if n >= 3:
                    act.wait_ge(S["ffn_pe"], n - 2)
                act.activation(hid[:, n % 3, :], hid_ps[n % 3][:, :], ACT.Gelu, bias=b1_col[:, j:j + 1],
                               scale=alpha1[:, j:j + 1]).then_inc(S["hid_ok"], 1)

        @block.vector
        def _(dve):
            dve.memset(eps[:, :], RMS_EPS).then_inc(S["eps_ok"], 1)
            half = P // 2
            dve.memset(late_half[0:half, :], 0.0)
            dve.memset(late_half[half:P, :], 1.0 / GATE_NORMALIZER)
            dve.memset(early_half[0:half, :], 1.0 / GATE_NORMALIZER)
            dve.memset(early_half[half:P, :], 0.0)
            dve.memset(same_head[:, :], 0.0).then_inc(S["same_zero"], 1)
            dve.wait_ge(S["same_zero"], 1)
            for h in range(H):
                dve.memset(same_head[h * HP:(h + 1) * HP, h * E:(h + 1) * E], 1.0)
            dve.wait_ge(S["up_to_ok"], 1)
            dve.tensor_scalar(decay_sum[0:half, :], decay_sum[0:half, :], -1.0 / GATE_NORMALIZER, None, ALU.add)\
                .then_inc(S["consts_ok"], 1)

            def squares_x(b):
                dve.wait_ge(x_in[b], 16)
                for t in range(TB):
                    i = b * TB + t
                    ins = dve.tensor_tensor_reduce(xh[:, i, :], xs[:, i, :], xs[:, i, :], 1.0, 0.0, ALU.mult,
                                                   ALU.add, x_ssq[:, i:i + 1])
                ins.then_inc(S["xssq_ok"], 1)

            def scale_x(b):
                dve.wait_ge(S["xrs_ok"], b + 1)
                for t in range(TB):
                    i = b * TB + t
                    ins = dve.tensor_scalar(xh[:, i, :], xs[:, i, :], x_rs[:, i:i + 1], None, ALU.mult)
                ins.then_inc(S["xh_ok"], 1)

            def z_start(b):
                dve.wait_ge(S["qkz_pe"], b + 1)
                bias = z_bias[:, :].unsqueeze(1).to_broadcast([P, TB, DK])
                if b >= 1:
                    dve.wait_ge(S["glog_ok"], b)
                dve.tensor_tensor(zb[:, :, :], qkz_ps[:, :, 2 * DK:QKZ], bias, ALU.add).then_inc(S["zb_ok"], 1)
                dve.wait_ge(S["zb_ok"], b + 1)
                if b >= 1:
                    dve.wait_ge(S["ze_ok"], b)
                dve.scalar_tensor_tensor(out=z_na[:, :, :], in0=zb[:, :, :], scalar=-1.0, in1=zb[:, :, :],
                                         op0=ALU.mult, op1=ALU.min).then_inc(S["zna_ok"], 1)

            def z_end(b):
                dve.wait_ge(S["zl_ok"], b + 1)
                if b == 0:
                    dve.wait_ge(S["pads_ok"], 1)
                if b >= 2:
                    dve.wait_ge(S["carry_pe"], b - 1)
                g4 = glog[:, b % 2].rearrange("p t (h d) -> p (t h) d", d=HP)[:, :, 0:HD]
                dve.scalar_tensor_tensor(out=g4, in0=zb[:, :, :].rearrange("p t (h d) -> p (t h) d", d=HD),
                                         scalar=0.0, in1=z_l[:, :, :].rearrange("p t (h d) -> p (t h) d", d=HD),
                                         op0=ALU.min, op1=ALU.subtract).then_inc(S["glog_ok"], 1)

            def g_start(b):
                dve.wait_ge(S["vg_ok"], b + 1)
                if b >= 1:
                    dve.wait_ge(S["ge_ok"], b)
                dve.scalar_tensor_tensor(out=g_na[:, :, :], in0=vg[:, tiles(b), DV:VG], scalar=-1.0,
                                         in1=vg[:, tiles(b), DV:VG], op0=ALU.mult, op1=ALU.min)\
                    .then_inc(S["gna_ok"], 1)

            def g_end(b):
                dve.wait_ge(S["gl_ok"], b + 1)
                if b >= 1:
                    dve.wait_ge(S["gsg_ok"], b)
                dve.scalar_tensor_tensor(out=g_ls[:, :, :], in0=vg[:, tiles(b), DV:VG], scalar=0.0,
                                         in1=g_l[:, :, :], op0=ALU.min, op1=ALU.subtract).then_inc(S["gls_ok"], 1)

            def scale_qk(b):
                if b >= 2:
                    dve.wait_ge(S["turn_pe"], b - 1)
                    dve.wait_ge(S["kv_pe"], b - 1)

                def heads(ap, width):
                    return ap.rearrange("p t (h d) -> p t h d", d=width)[:, :, :, 0:HD]
                dve.wait_ge(S["grow_ok"], b + 1)
                q_in = heads(qkz_ps[:, :, 0:DK], HD)
                k_in = heads(qkz_ps[:, :, DK:2 * DK], HD)
                g_in = grow[:, :].rearrange("p (t h d) -> p t h d", t=TB, h=H)
                f_in = fall[:, :].rearrange("p (t h d) -> p t h d", t=TB, h=H)
                dve.wait_ge(S["fall_ok"], b + 1)
                dve.tensor_tensor(heads(qe[:, b % 2], HP), q_in, g_in, ALU.mult).then_inc(S["qe_ok"], 1)
                dve.tensor_tensor(heads(ke[:, b % 2], HP), k_in, f_in, ALU.mult).then_inc(S["ke_ok"], 1)

            def mask(b, t):
                dve.wait_ge(S["a_pe"], TB * b + t + 1)
                if b == 0:
                    dve.wait_ge(S["pads_ok"], 2)
                if b >= 2:
                    dve.wait_ge(S["o_pe"], b - 1)
                dve.copy_predicated(att[:, b % 2, t, :], causal[:, :].bitcast(U32), bank_a[t][:, :])\
                    .then_inc(S["att_ok"], 1)

            def make_state(b):
                dve.wait_ge(S["kv_pe"], b + 1)
                dve.wait_ge(S["carry_ok"], b + 1)
                if b == 0:
                    dve.wait_ge(S["consts_ok"], 1)
                if b >= 2:
                    dve.wait_ge(S["o_pe"], b - 1)
                dve.scalar_tensor_tensor(out=state[:, b % 2, :], in0=kv_ps, scalar=carry[:, b % 2, 0:1],
                                         in1=same_head[:, :], op0=ALU.mult, op1=ALU.mult)\
                    .then_inc(S["kv_ok"], 1)

            def norm_o(b):
                dve.wait_ge(S["osq_ok"], b + 1)
                dve.tensor_reduce(o_ssq[:, tiles(b), :], o_sq[:, b % 2].rearrange("p t (h e) -> p t h e", e=E),
                                  AX.X, ALU.add).then_inc(S["ossq_ok"], 1)

            def gated(b):
                dve.wait_ge(S["ors_ok"], b + 1)
                rs = o_rs[:, tiles(b), :].unsqueeze(3).to_broadcast([P, TB, H, E])
                if b >= 1:
                    dve.wait_ge(S["og_ok"], b)
                dve.tensor_tensor(o_n[:, :, :].rearrange("p t (h e) -> p t h e", e=E),
                                  o_sb[:, b % 2].rearrange("p t (h e) -> p t h e", e=E), rs, ALU.mult)\
                    .then_inc(S["on_ok"], 1)
                dve.wait_ge(S["on_ok"], b + 1)
                dve.wait_ge(S["gs_ok"], b + 1)
                if b >= 2:
                    dve.wait_ge(S["ogT_pe"], b - 1)
                dve.tensor_tensor(og[:, b % 2], o_n[:, :, :], gs[:, b % 2], ALU.mult).then_inc(S["og_ok"], 1)

            def residual(b):
                dve.wait_ge(S["wo_pe"], b + 1)
                dve.tensor_tensor(x2[:, tiles(b), :], wo_ps, xs[:, tiles(b), :], ALU.add).then_inc(S["x2_ok"], 1)
                dve.wait_ge(S["x2_ok"], b + 1)
                for t in range(TB):
                    i = b * TB + t
                    ins = dve.tensor_tensor_reduce(y[:, i, :], x2[:, i, :], x2[:, i, :], 1.0, 0.0, ALU.mult,
                                                   ALU.add, x2_ssq[:, i:i + 1])
                ins.then_inc(S["x2ssq_ok"], 1)

            def scale_x2(b):
                dve.wait_ge(S["x2rs_ok"], b + 1)
                if b >= 2:
                    dve.wait_ge(S["ogT_pe"], b)
                for t in range(TB):
                    i = b * TB + t
                    ins = dve.tensor_scalar(n_sb[:, b % 2, t, :], x2[:, i, :], x2_rs[:, i:i + 1], None, ALU.mult)
                ins.then_inc(S["n_ok"], 1)

            squares_x(0)
            scale_x(0)
            dve.wait_ge(gk_in, 48)
            dve.wait_ge(S["gk1T_ps"], 1)
            dve.tensor_copy(gk1T[:, :], bank_uw[0:R, 0:P]).then_inc(S["gk1T_ok"], 1)
            dve.wait_ge(attn_w_in, 80)
            dve.tensor_scalar(w_qkz[:, 0:DK], w_in[:, 0:DK], anw[:, 0:1], float(HD) ** -0.5, ALU.mult, ALU.mult)\
                .then_inc(S["w_attn_ok"], 1)
            dve.tensor_scalar(w_qkz[:, DK:2 * DK], w_in[:, DK:2 * DK], anw[:, 0:1], None, ALU.mult)
            dve.tensor_scalar(w_vg[:, :], w_in[:, 2 * DK:2 * DK + VG], anw[:, 0:1], None, ALU.mult)\
                .then_inc(S["w_attn_ok"], 1)
            dve.wait_ge(S["gkw_ps"], 1)
            dve.tensor_scalar(w_qkz[:, 2 * DK:QKZ], bank_uw[:, 0:DK], anw[:, 0:1], None, ALU.mult)\
                .then_inc(S["w_attn_ok"], 1)
            squares_x(1)
            scale_x(1)
            squares_x(2)

            def prepare_o():
                dve.wait_ge(wo_w_in, 16 * (1 + H))
                dve.tensor_scalar(w_o[:, :], wo_in[:, :], gnw[:, 0:1], None, ALU.mult).then_inc(S["w_o_ok"], 1)

            def prepare_mlp():
                dve.wait_ge(mlp_w_in, 48)
                dve.tensor_scalar(w_gu[:, :], gu_in[:, :], mnw[:, 0:1], None, ALU.mult).then_inc(S["w_gu_ok"], 1)

            def prepare_ffn():
                dve.wait_ge(ffn_w_in, 64)
                dve.tensor_scalar(neg1[:, :, :], w1_in[:, :, :], 0.0, None, ALU.is_lt).then_inc(S["half1_ok"], 1)
                dve.tensor_scalar(neg2[:, :], w2_in[:, :], 0.0, None, ALU.is_lt).then_inc(S["half2_ok"], 1)
                dve.wait_ge(S["half1_ok"], 1)
                dve.scalar_tensor_tensor(out=sign1[:, :, :], in0=w1_in[:, :, :], scalar=0.0, in1=neg1[:, :, :],
                                         op0=ALU.is_gt, op1=ALU.subtract).then_inc(S["sign1_ok"], 1)
                dve.wait_ge(S["half2_ok"], 1)
                dve.scalar_tensor_tensor(out=sign2[:, :], in0=w2_in[:, :], scalar=0.0, in1=neg2[:, :],
                                         op0=ALU.is_gt, op1=ALU.subtract).then_inc(S["sign2_ok"], 1)

            def prepare_alpha():
                dve.tensor_reduce(abs1[:, :], w1_in[:, :, :], AX.X, ALU.add, apply_absolute_value=True)
                dve.tensor_reduce(abs2[:, :], w2_in[:, :], AX.X, ALU.add, apply_absolute_value=True)\
                    .then_inc(S["abs_ok"], 1)
                dve.wait_ge(S["abs_ok"], 1)
                dve.tensor_scalar(alpha1[:, :], abs1[:, :], 1.0 / D, None, ALU.mult).then_inc(S["alpha_ok"], 1)
                dve.tensor_scalar(alpha2[:, :], abs2[:, :], 1.0 / HF, None, ALU.mult).then_inc(S["alpha_ok"], 1)
                dve.wait_ge(S["alpha_ok"], 2)
                dve.wait_ge(S["sign2_ok"], 1)
                dve.tensor_scalar(bin2[:, :], sign2[:, :], alpha2[:, 0:1], None, ALU.mult).then_inc(S["bin2_ok"], 1)

            for k in range(-2, NB + 2):
                if 0 <= k + 1 < NB:
                    z_start(k + 1)
                if 0 <= k < NB:
                    mask(k, 0)
                if 0 <= k + 1 < NB:
                    z_end(k + 1)
                    g_start(k + 1)
                if 0 <= k < NB:
                    make_state(k)
                    mask(k, 1)
                if 0 <= k - 2 < NB - 1:
                    scale_x2(k - 2)
                if 0 <= k + 1 < NB:
                    g_end(k + 1)
                    scale_qk(k + 1)
                if 0 <= k + 4 < NB:
                    scale_x(k + 4)
                if 0 <= k < NB:
                    norm_o(k)
                if 0 <= k - 1 < NB:
                    residual(k - 1)
                if k == NB:
                    scale_x2(NB - 1)
                if 0 <= k + 5 < NB:
                    squares_x(k + 5)
                if 0 <= k < NB:
                    gated(k)
                if k == -1:
                    prepare_o()
                if k == 0:
                    prepare_mlp()
                if k == 1:
                    prepare_ffn()
                if k == 2:
                    prepare_alpha()

            def layer_norm(c, which, source, source_sem, source_value, addend, dest, done):
                q = c % 2
                dve.wait_ge(S[source_sem], source_value)
                dve.tensor_tensor(ln_in[:, q], source[:, :].rearrange("p (t d) -> p t d", t=TC), addend, ALU.add)\
                    .then_inc(S["t" + which], 1)
                dve.wait_ge(S["t" + which], c + 1)
                for t in range(TC):
                    ins = dve.bn_stats(ln_st[:, q, t, :], ln_in[:, q, t, :])
                ins.then_inc(S["st" + which], 1)
                dve.wait_ge(S["st" + which], c + 1)
                for t in range(TC):
                    ins = dve.bn_aggr(ln_mv[:, q, t, :], ln_st[:, q, t, :])
                ins.then_inc(S["mv" + which], 1)

            def normalize(c, which, dest, done):
                q = c % 2
                dve.wait_ge(S["rs" + which], c + 1)
                for t in range(TC):
                    ins = dve.tensor_scalar(dest(t), ln_in[:, q, t, :], ln_mv[:, q, t, 0:1], ln_rs[:, q, t:t + 1],
                                            ALU.subtract, ALU.mult)
                ins.then_inc(S[done], 1)

            def gated_up(n):
                j = n % NI
                dve.wait_ge(S["up_pe"], n + 1)
                dve.wait_ge(S["gates_ok"], n + 1)
                if n >= 3:
                    dve.wait_ge(S["down_pe"], n - 2)
                dve.tensor_tensor(act_T[0:IW[j], n % 3, :], up_ps[n % 2][0:IW[j], :], gate_s[0:IW[j], n % 2, :],
                                  ALU.mult).then_inc(S["act_ok"], 1)

            def norm1(c):
                dve.wait_ge(S["xx2_ok"], (c + 1) * TC // TB)
                layer_norm(c, "1_ok", down_ps, "down_pe", NI * (c + 1), xx2[:, ctiles(c), :], None, None)

            for n in range(NC * NI + 2):
                if n < NC * NI:
                    gated_up(n)
                if n >= 4 and n % NI == 1:
                    norm1(n // NI - 1)
                if n >= 5 and n % NI == 2:
                    c = n // NI - 1
                    normalize(c, "1_ok", lambda t, c=c: y[:, c * TC + t, :], "y_ok")
            c = NC - 1
            normalize(c, "1_ok", lambda t, c=c: y[:, c * TC + t, :], "y_ok")

            def low_y(c):
                dve.wait_ge(S["yhi_ok"], c + 1)
                if c >= 2:
                    dve.wait_ge(S["hid_pe"], NF * (c - 1))
                dve.tensor_tensor(y_lo[:, c % 2, :], yT_ps[:, :], y_hi[:, c % 2, :].bitcast(F32), ALU.subtract)\
                    .then_inc(S["ylo_ok"], 1)

            low_y(0)
            for c in range(NC):
                if c + 1 < NC:
                    low_y(c + 1)
                dve.wait_ge(S["yb_ok"], c + 1)
                layer_norm(c, "2_ok", ffn_ps[c % 2], "ffn_pe", NF * (c + 1), yb[:, ctiles(c), :], None, None)
                normalize(c, "2_ok", lambda t, c=c: y_out[:, c * TC + t, :], "yout_ok")


_INS = ['L0_attn_hidden_states', 'L0_attn_attn_norm_w', 'L0_attn_Wq', 'L0_attn_Wk', 'L0_attn_Wv', 'L0_attn_Wg',
        'L0_attn_Wgk1', 'L0_attn_Wgk2', 'L0_attn_bgk2', 'L0_attn_gnorm_w', 'L0_attn_Wo', 'L0_attn_mlp_norm_w',
        'L0_attn_W_gate', 'L0_attn_W_up', 'L0_attn_W_down', 'L0_ffn_w1', 'L0_ffn_b1', 'L0_ffn_w2', 'L0_ffn_b2']


def kernel(**inputs):
    import numpy as np
    import concourse.bacc as bacc
    from concourse.bass_utils import run_bass_kernel_spmd

    nc = bacc.Bacc("TRN2", target_bir_lowering=False, num_devices=1)
    arrays, args = {}, []
    for name in _INS:
        a = np.ascontiguousarray(inputs[name])
        arrays[f"in_{name}_dram"] = a
        args.append(nc.dram_tensor(f"in_{name}_dram", a.shape, mybir.dt.from_np(a.dtype), kind="ExternalInput").ap())
    shape = inputs['L0_attn_hidden_states'].shape
    args.append(nc.dram_tensor("out_dram", shape, F32, kind="ExternalOutput").ap())
    gla_block_and_binary_ffn(nc, *args)
    result = run_bass_kernel_spmd(nc, [arrays], core_ids=[0])
    return result.results[0]["out_dram"]
```

```python
from contextlib import ExitStack

import concourse.bass as bass
from concourse import mybir

F32 = mybir.dt.float32
F32R = mybir.dt.float32r
U32 = mybir.dt.uint32
ALU = mybir.AluOpType
ACT = mybir.ActivationFunctionType
AX = mybir.AxisListType

P = 128
RMS_EPS = 1e-6
LN_EPS = 1e-5
GATE_NORMALIZER = 16.0
BATCH_TILES = 2
CHUNK_TILES = 4


def gla_block_and_binary_ffn(nc, x, attn_norm_w, Wq, Wk, Wv, Wg, Wgk1, Wgk2, bgk2, gnorm_w, Wo,
                             mlp_norm_w, W_gate, W_up, W_down, w1, b1, w2, b2, out):
    B, T, D = x.shape
    DK = Wq.shape[1]
    DV = Wv.shape[1]
    R = Wgk1.shape[1]
    E = gnorm_w.shape[0]
    H = DV // E
    HD = DK // H
    HP = P // H
    I = W_gate.shape[1]
    HF = w1.shape[0]
    NB, TB, TC = B, BATCH_TILES, CHUNK_TILES
    NT = B * T // P
    NC = NT // TC
    CH = TC * P
    BT = TB * P
    NI = -(-I // P)
    NF = HF // P
    IW = [min(P, I - j * P) for j in range(NI)]
    QKZ, VG = 2 * DK + DK, 2 * DV
    assert T == BT and D == P and DV == P and H * HP == P and HD <= HP and E == HP
    assert TB * QKZ <= 512 and TB * VG <= 512 and TB * H * P <= 1024 and CH == 512

    with ExitStack() as ctx:
        def sb(name, shape, dt=F32):
            return ctx.enter_context(nc.sbuf_tensor(name, shape, dt))

        def bank(name):
            return ctx.enter_context(nc.psum_tensor(name, [P, 512], F32))

        def sem(name):
            return ctx.enter_context(nc.semaphore(name))

        bank_qkz, bank_vg, bank_turn = bank("bank_qkz"), bank("bank_vg"), bank("bank_turn")
        bank_a = [bank("bank_a0"), bank("bank_a1")]
        bank_o, bank_dx, bank_uw = bank("bank_o"), bank("bank_dx"), bank("bank_uw")
        qkz_ps = bank_qkz[:, 0:TB * QKZ].rearrange("p (t n) -> p t n", t=TB)
        vg_ps = bank_vg[:, :].rearrange("p (t n) -> p t n", t=TB)
        o_ps = bank_o[:, 0:TB * DV].rearrange("p (t n) -> p t n", t=TB)
        xT_ps = bank_dx[:, 0:BT]
        decay_ps = bank_dx[:, BT:BT + TB * DK]
        carry_ps = bank_dx[:, BT + TB * DK:BT + TB * DK + 2]
        kv_ps = bank_uw[:, 0:DV]
        wo_ps = bank_uw[:, DV:DV + TB * D].rearrange("p (t n) -> p t n", t=TB)
        gate_ps = [bank_turn, bank_qkz]
        up_ps = bank_a
        down_ps = [bank_o, bank_vg]
        signs_ps = yT_ps = bank_dx
        hid_ps = [bank_uw, bank_turn, bank_qkz]

        def ffn_ps(c, t):
            if c < NC - 1:
                return bank_a[c % 2][:, t * P:(t + 1) * P]
            return [bank_a[1], bank_o, bank_vg, bank_dx][t][:, 0:P]

        ident = sb("ident", [P, P])
        causal = sb("causal", [P, H * P])
        decay_sum = sb("decay_sum", [P, P])
        late_half = sb("late_half", [P, 2])
        early_half = sb("early_half", [P, 2])
        same_head = sb("same_head", [P, DV])
        eps = sb("eps", [P, 1])
        minus_half = sb("minus_half", [P, TC])
        w_in = sb("w_in", [P, 2 * DK + 2 * DV])
        anw = sb("anw", [P, 1])
        gk1_in = sb("gk1_in", [P, R])
        gk2_in = sb("gk2_in", [R, DK])
        z_bias = sb("z_bias", [P, DK])
        wo_in = sb("wo_in", [P, D])
        gnw = sb("gnw", [P, 1])
        mnw = sb("mnw", [P, 1])
        gu_in = sb("gu_in", [P, 2 * I])
        w1_in = sb("w1_in", [P, NF, D])
        w2_in = sb("w2_in", [P, HF])
        b1_col = sb("b1_col", [P, NF])
        b2_row = sb("b2_row", [P, D])
        gk1T = sb("gk1T", [R, P])
        w_qkz = sb("w_qkz", [P, QKZ])
        w_vg = sb("w_vg", [P, VG])
        w_o = sb("w_o", [P, D])
        w_gu = sb("w_gu", [P, 2 * I])
        w_down = sb("w_down", [P, NI, D])
        neg1 = sb("neg1", [P, NF, D])
        sign1 = sb("sign1", [P, NF, D])
        neg2 = sb("neg2", [P, HF])
        sign2 = sb("sign2", [P, HF])
        bin2 = sb("bin2", [P, HF])
        abs1 = sb("abs1", [P, NF])
        alpha1 = sb("alpha1", [P, NF])
        abs2 = sb("abs2", [P, 1])
        alpha2 = sb("alpha2", [P, 1])
        sign1T = sb("sign1T", [P, HF], F32R)
        bin2T = sb("bin2T", [P, NF, D])
        xs = sb("xs", [P, NT, D])
        x_ssq = sb("x_ssq", [P, NT])
        x_ln = sb("x_ln", [P, NT])
        x_rs = sb("x_rs", [P, NT])
        xh = sb("xh", [P, NT, D])
        xT = sb("xT", [P, NT * P])
        zb = sb("zb", [P, TB, DK])
        z_na = sb("z_na", [P, TB, DK])
        z_e = sb("z_e", [P, TB, DK])
        z_l = sb("z_l", [P, TB, DK])
        glog = sb("glog", [P, 2, TB, P])
        vg = sb("vg", [P, NT, VG])
        g_na = sb("g_na", [P, TB, DV])
        g_e = sb("g_e", [P, TB, DV])
        g_l = sb("g_l", [P, TB, DV])
        g_ls = sb("g_ls", [P, TB, DV])
        g_sg = sb("g_sg", [P, TB, DV])
        gs = sb("gs", [P, 2, TB, DV])
        grow = sb("grow", [P, TB * DK])
        fall = sb("fall", [P, TB * DK])
        carry = sb("carry", [P, 2, 2])
        qe = sb("qe", [P, 2, TB, P])
        ke = sb("ke", [P, 2, TB, P])
        kT = sb("kT", [P, 2, BT])
        qT1 = sb("qT1", [P, 2, P])
        qheads = sb("qheads", [P, 2, TB, H, P])
        att = sb("att", [P, 2, TB, H * P])
        state = sb("state", [P, 2, DV])
        o_sb = sb("o_sb", [P, 2, TB, DV])
        o_sq = sb("o_sq", [P, 2, TB, DV])
        o_ssq = sb("o_ssq", [P, NT, H])
        o_ln = sb("o_ln", [P, NT, H])
        o_rs = sb("o_rs", [P, NT, H])
        o_n = sb("o_n", [P, TB, DV])
        og = sb("og", [P, 2, TB, DV])
        onT = sb("onT", [P, NB + 1, 2, BT])
        x2 = sb("x2", [P, NT, D])
        x2_ssq = sb("x2_ssq", [P, NT])
        x2_ve = sb("x2_ve", [P, NT])
        x2_rs = sb("x2_rs", [P, NT])
        n_sb = sb("n_sb", [P, 2, TB, D])
        xx2 = sb("xx2", [P, NT, D])
        gate_s = sb("gate_s", [P, 2, CH])
        act_T = sb("act_T", [P, 3, CH])
        ln_in = sb("ln_in", [P, 2, TC, D])
        ln_st = sb("ln_st", [P, 2, TC, 6])
        ln_mv = sb("ln_mv", [P, 2, TC, 2])
        ln_ve = sb("ln_ve", [P, 2, TC])
        ln_rs = sb("ln_rs", [P, 2, TC])
        y = sb("y", [P, NT, D])
        yb = sb("yb", [P, NT, D])
        y_hi = sb("y_hi", [P, 2, CH], F32R)
        y_lo = sb("y_lo", [P, 2, CH], F32R)
        hid = sb("hid", [P, 3, CH])
        y_out = sb("y_out", [P, NT, D])

        x_in = [sem(f"x_in{b}") for b in range(NB)]
        attn_w_in, gk_in, wo_w_in, mlp_w_in = sem("attn_w_in"), sem("gk_in"), sem("wo_w_in"), sem("mlp_w_in")
        down_w_in, ffn_w_in, out_done = sem("down_w_in"), sem("ffn_w_in"), sem("out_done")
        names = """eps_ok ident_ok consts_zero up_to_ok same_zero consts_ok pads_ok gk1T_ps gk1T_ok gkw_ps w_attn_ok w_o_ok w_gu_ok
            half1_ok sign1_ok half2_ok sign2_ok abs_ok alpha_ok bin2_ok sign1T_ps sign1T_ok bin2T_ps bin2T_ok
            xssq_ok xln_ok xrs_ok xh_ok xT_pe xT_ok qkz_pe vg_pe vg_ok zb_ok zna_ok ze_ok zl_ok glog_ok
            gna_ok ge_ok gl_ok gls_ok gsg_ok gs_ok carry_pe grow_ok fall_ok carry_ok qe_ok ke_ok
            turn_pe kT_ok qheads_ok a_pe att_ok kv_pe kv_ok o_pe o_ok osq_ok ossq_ok oln_ok ors_ok
            on_ok og_ok ogT_pe onT_ok wo_pe x2_ok x2ssq_ok x2ve_ok x2rs_ok n_ok xx2_ok
            gate_pe up_pe gates_ok act_ok down_pe half_ok t1_ok st1_ok mv1_ok ve1_ok rs1_ok y_ok yb_ok
            yT_pe yhi_ok ylo_ok hid_pe hid_ok ffn_pe t2_ok st2_ok mv2_ok ve2_ok rs2_ok yout_ok""".split()
        S = {n: sem(n) for n in names}

        def tiles(b):
            return slice(b * TB, (b + 1) * TB)

        def ctiles(c):
            return slice(c * TC, (c + 1) * TC)

        steps2 = [(c, 0, TC) for c in range(NC - 1)] + [(NC - 1, t, t + 1) for t in range(TC)]

        block = ctx.enter_context(nc.Block())

        @block.sync
        def _(sp):
            xv = x.rearrange("b (t p) d -> p (b t) d", p=P)
            ov = out.rearrange("b (t p) d -> p (b t) d", p=P)
            sp.dma_start(xs[:, tiles(0), :], xv[:, tiles(0), :]).then_inc(x_in[0], 16)
            sp.dma_start(w_in[:, 0:DK], Wq).then_inc(attn_w_in, 16)
            sp.dma_start(w_in[:, DK:2 * DK], Wk).then_inc(attn_w_in, 16)
            sp.dma_start(xs[:, tiles(1), :], xv[:, tiles(1), :]).then_inc(x_in[1], 16)
            sp.dma_start(xs[:, tiles(2), :], xv[:, tiles(2), :]).then_inc(x_in[2], 16)
            sp.dma_start(wo_in[:, :], Wo).then_inc(wo_w_in, 16)
            for h in range(H):
                sp.dma_start(gnw[h * E:(h + 1) * E, :], gnorm_w.rearrange("(e a) -> e a", a=1)).then_inc(wo_w_in, 16)
            for b in range(3, NB):
                sp.dma_start(xs[:, tiles(b), :], xv[:, tiles(b), :]).then_inc(x_in[b], 16)
            sp.dma_start(gu_in[:, 0:I], W_gate).then_inc(mlp_w_in, 16)
            sp.dma_start(gu_in[:, I:2 * I], W_up).then_inc(mlp_w_in, 16)
            sp.dma_start(mnw[:, :], mlp_norm_w.rearrange("(p a) -> p a", a=1)).then_inc(mlp_w_in, 16)
            sp.dma_start(w1_in[:, :, :], w1.rearrange("(p j) d -> p j d", p=P)).then_inc(ffn_w_in, 16)
            sp.dma_start(w2_in[:, :], w2).then_inc(ffn_w_in, 16)
            sp.dma_start(b1_col[:, :], b1.rearrange("(p j) -> p j", p=P)).then_inc(ffn_w_in, 16)
            sp.dma_start(b2_row[:, :], b2.partition_broadcast(P)).then_inc(ffn_w_in, 16)
            for j in range(NI):
                sp.dma_start(w_down[0:IW[j], j, :], W_down[j * P:j * P + IW[j], :]).then_inc(down_w_in, 16)
            for g, (c, a, z) in enumerate(steps2):
                i, e = c * TC + a, c * TC + z
                sp.wait_ge(S["yout_ok"], g + 1)
                sp.dma_start(ov[:, i:e, :], y_out[:, i:e, :]).then_inc(out_done, 16)
            sp.wait_ge(out_done, 16 * len(steps2))

        @block.gpsimd
        def _(pool):
            pool.dma_start(gk1_in[:, :], Wgk1).then_inc(gk_in, 16)
            pool.dma_start(gk2_in[:, :], Wgk2).then_inc(gk_in, 16)
            pool.dma_start(z_bias[:, :], bgk2.partition_broadcast(P)).then_inc(gk_in, 16)
            pool.memset(ident[:, :], 0.0)
            pool.memset(decay_sum[:, :], 0.0)
            pool.memset(causal[:, :], 0.0).then_inc(S["consts_zero"], 1)
            pool.wait_ge(S["consts_zero"], 1)
            pool.affine_select(out=ident[:, :], in_=ident[:, :], compare_op=ALU.not_equal, fill=1.0, base=0,
                               pattern=[[-1, P]], channel_multiplier=1).then_inc(S["ident_ok"], 1)
            pool.affine_select(out=decay_sum[:, :], in_=decay_sum[:, :], compare_op=ALU.is_gt,
                               fill=1.0 / GATE_NORMALIZER, base=0, pattern=[[-1, P]], channel_multiplier=1)\
                .then_inc(S["up_to_ok"], 1)
            pool.memset(glog[:, :, :, :], 0.0)
            pool.memset(qe[:, :, :, :], 0.0)
            pool.memset(ke[:, :, :, :], 0.0)
            pool.memset(qheads[:, :, :, :, :], 0.0).then_inc(S["pads_ok"], 1)
            pool.affine_select(out=causal[:, :], in_=causal[:, :], compare_op=ALU.is_gt, fill=1.0, base=0,
                               pattern=[[0, H], [-1, P]], channel_multiplier=1)
            pool.memset(att[:, :, :, :], 0.0).then_inc(S["pads_ok"], 1)
            pool.memset(minus_half[:, :], -0.5).then_inc(S["half_ok"], 1)

            def gate_product(b):
                pool.wait_ge(S["gsg_ok"], b + 1)
                pool.wait_ge(S["vg_ok"], b + 1)
                if b >= 2:
                    pool.wait_ge(S["og_ok"], b - 1)
                pool.tensor_tensor(gs[:, b % 2], vg[:, tiles(b), DV:VG], g_sg[:, :, :], ALU.mult).then_inc(S["gs_ok"], 1)

            def o_squares(b):
                pool.wait_ge(S["o_ok"], b + 1)
                if b >= 2:
                    pool.wait_ge(S["ossq_ok"], b - 1)
                pool.tensor_tensor(o_sq[:, b % 2], o_sb[:, b % 2], o_sb[:, b % 2], ALU.mult).then_inc(S["osq_ok"], 1)

            def x_plus_x2(b):
                pool.wait_ge(S["x2_ok"], b + 1)
                pool.tensor_tensor(xx2[:, tiles(b), :], xs[:, tiles(b), :], x2[:, tiles(b), :], ALU.add)\
                    .then_inc(S["xx2_ok"], 1)

            def root_x2(b):
                pool.wait_ge(S["x2ssq_ok"], b + 1)
                pool.tensor_scalar(x2_ve[:, tiles(b)], x2_ssq[:, tiles(b)], 1.0 / D, RMS_EPS, ALU.mult, ALU.add)\
                    .then_inc(S["x2ve_ok"], 1)
                pool.wait_ge(S["x2ve_ok"], b + 1)
                pool.tensor_tensor(x2_rs[:, tiles(b)], x2_ve[:, tiles(b)], minus_half[:, 0:TB], ALU.pow)\
                    .then_inc(S["x2rs_ok"], 1)

            pool.wait_ge(S["half_ok"], 1)
            for k in range(-1, NB + 1):
                if 0 <= k < NB:
                    o_squares(k)
                if 0 <= k + 1 < NB:
                    gate_product(k + 1)
                if 0 <= k - 1 < NB:
                    root_x2(k - 1)
                    x_plus_x2(k - 1)

            def root_var(mv, ve, rs, which, g):
                pool.wait_ge(S["mv" + which], g + 1)
                pool.tensor_scalar(ve, mv, LN_EPS, 1.0, ALU.add, ALU.mult).then_inc(S["ve" + which], 1)
                pool.wait_ge(S["ve" + which], g + 1)
                pool.tensor_tensor(rs, ve, minus_half[:, 0:ve.shape[1]], ALU.pow).then_inc(S["rs" + which], 1)

            pool.wait_ge(ffn_w_in, 64)
            for c in range(NC):
                root_var(ln_mv[:, c % 2, :, 1], ln_ve[:, c % 2], ln_rs[:, c % 2], "1_ok", c)
                pool.wait_ge(S["y_ok"], c + 1)
                for t in range(TC):
                    i = c * TC + t
                    ins = pool.tensor_tensor(yb[:, i, :], y[:, i, :], b2_row[:, :], ALU.add)
                ins.then_inc(S["yb_ok"], 1)
            for g, (c, a, z) in enumerate(steps2):
                root_var(ln_mv[:, c % 2, a:z, 1], ln_ve[:, c % 2, a:z], ln_rs[:, c % 2, a:z], "2_ok", g)

        @block.tensor
        def _(pe):
            def turn_x(b):
                pe.wait_ge(S["xh_ok"], b + 1)
                if b >= 1:
                    pe.wait_ge(S["xT_ok"], b)
                if b >= 2:
                    pe.wait_ge(S["carry_ok"], b - 1)
                for t in range(TB):
                    ins = pe.transpose(xT_ps[:, t * P:(t + 1) * P], xh[:, b * TB + t, :], ident[:, :])
                ins.then_inc(S["xT_pe"], 1)

            def project(b):
                if b == 0:
                    pe.wait_ge(S["w_attn_ok"], 3)
                pe.wait_ge(S["xT_ok"], b + 1)
                if b >= 1:
                    pe.wait_ge(S["ke_ok"], b)
                for t in range(TB):
                    i = b * TB + t
                    ins = pe.matmul(qkz_ps[:, t, :], xT[:, i * P:(i + 1) * P], w_qkz[:, :], start=True, stop=True)
                ins.then_inc(S["qkz_pe"], 1)
                if b >= 1:
                    pe.wait_ge(S["vg_ok"], b)
                if b >= 3:
                    pe.wait_ge(S["onT_ok"], b - 2)
                for t in range(TB):
                    i = b * TB + t
                    ins = pe.matmul(vg_ps[:, t, :], xT[:, i * P:(i + 1) * P], w_vg[:, :], start=True, stop=True)
                ins.then_inc(S["vg_pe"], 1)

            def decay(b):
                pe.wait_ge(S["glog_ok"], b + 1)
                if b >= 1:
                    pe.wait_ge(S["carry_ok"], b)
                pe.wait_ge(S["xT_ok"], min(b + 2, NB))
                g4 = glog[:, b % 2].rearrange("p t (h d) -> p (t h) d", d=HP)[:, :, 0:HD]
                pe.matmul(decay_ps, decay_sum[:, :], g4, start=True, stop=True)
                pe.matmul(carry_ps, glog[:, b % 2, 0, :], late_half[:, :], start=True, stop=False)
                pe.matmul(carry_ps, glog[:, b % 2, 1, :], early_half[:, :], start=False, stop=True)\
                    .then_inc(S["carry_pe"], 1)

            def turn_qk(b):
                pe.wait_ge(S["qe_ok"], b + 1)
                pe.wait_ge(S["ke_ok"], b + 1)
                if b >= 1:
                    pe.wait_ge(S["qheads_ok"], b)
                for t in range(TB):
                    pe.transpose(bank_turn[:, t * P:(t + 1) * P], ke[:, b % 2, t, :], ident[:, :])
                for t in range(TB):
                    ins = pe.transpose(bank_turn[:, BT + t * P:BT + (t + 1) * P], qe[:, b % 2, t, :], ident[:, :])
                ins.then_inc(S["turn_pe"], 1)

            def scores(b):
                pe.wait_ge(S["kT_ok"], b + 1)
                pe.wait_ge(S["qheads_ok"], b + 1)
                for t in range(TB):
                    if b >= 1:
                        pe.wait_ge(S["att_ok"], TB * (b - 1) + t + 1)
                    pe.matmul(bank_a[t][:, :], kT[:, b % 2, t * P:(t + 1) * P],
                              qheads[:, b % 2, t].rearrange("p h c -> p (h c)"),
                              start=True, stop=True).then_inc(S["a_pe"], 1)

            def key_values(b):
                if b >= 2:
                    pe.wait_ge(S["x2_ok"], b - 1)
                pe.matmul(kv_ps, ke[:, b % 2, 0, :], vg[:, b * TB, 0:DV], start=True, stop=True)\
                    .then_inc(S["kv_pe"], 1)

            def outputs(b, t):
                pe.wait_ge(S["att_ok"], TB * b + t + 1)
                if t == 0 and b >= 1:
                    pe.wait_ge(S["o_ok"], b)
                for h in range(H):
                    pe.matmul(o_ps[:, t, h * E:(h + 1) * E], att[:, b % 2, t, h * P:(h + 1) * P],
                              vg[:, b * TB + t, h * E:(h + 1) * E], start=(t == 0 and h == 0), stop=False,
                              skip_group_check=True)
                if t == 1:
                    pe.wait_ge(S["kv_ok"], b + 1)
                    pe.matmul(o_ps[:, 1, :], qT1[:, b % 2, :], state[:, b % 2, :], start=False, stop=True,
                              skip_group_check=True).then_inc(S["o_pe"], 1)

            def turn_og_n(s):
                if s < NB:
                    pe.wait_ge(S["og_ok"], s + 1)
                if s >= 1:
                    pe.wait_ge(S["n_ok"], s)
                    pe.wait_ge(S["onT_ok"], s)
                pe.wait_ge(S["vg_ok"], min(s + 2, NB))
                for t in range(TB):
                    if s < NB:
                        ins = pe.transpose(bank_vg[:, t * P:(t + 1) * P], og[:, s % 2, t, :], ident[:, :])
                for t in range(TB):
                    if s >= 1:
                        ins = pe.transpose(bank_vg[:, BT + t * P:BT + (t + 1) * P], n_sb[:, (s - 1) % 2, t, :],
                                           ident[:, :])
                ins.then_inc(S["ogT_pe"], 1)

            def project_out(b):
                if b == 0:
                    pe.wait_ge(S["w_o_ok"], 1)
                pe.wait_ge(S["onT_ok"], b + 1)
                pe.wait_ge(S["kv_ok"], min(b + 2, NB))
                if b >= 1:
                    pe.wait_ge(S["x2_ok"], b)
                for t in range(TB):
                    ins = pe.matmul(wo_ps[:, t, :], onT[:, b, 0, t * P:(t + 1) * P], w_o[:, :], start=True, stop=True)
                ins.then_inc(S["wo_pe"], 1)

            pe.wait_ge(S["ident_ok"], 1)
            pe.wait_ge(gk_in, 48)
            pe.transpose(bank_uw[0:R, 0:P], gk1_in[:, :], ident[:, :]).then_inc(S["gk1T_ps"], 1)
            pe.wait_ge(S["gk1T_ok"], 1)
            pe.matmul(bank_uw[:, 0:DK], gk1T[:, :], gk2_in[:, :], start=True, stop=True).then_inc(S["gkw_ps"], 1)
            pe.wait_ge(S["consts_ok"], 1)

            def turn_sign1():
                pe.wait_ge(S["sign1_ok"], 1)
                pe.wait_ge(S["xT_ok"], NB)
                pe.wait_ge(S["carry_ok"], NB)
                for j in range(NF):
                    ins = pe.transpose(signs_ps[:, j * P:(j + 1) * P], sign1[:, j, :], ident[:, :])
                ins.then_inc(S["sign1T_ps"], 1)

            def turn_bin2():
                pe.wait_ge(S["bin2_ok"], 1)
                pe.wait_ge(S["sign1T_ok"], 1)
                for j in range(NF):
                    ins = pe.transpose(signs_ps[:, j * P:(j + 1) * P], bin2[:, j:HF:NF], ident[:, :])
                ins.then_inc(S["bin2T_ps"], 1)

            def gate_up(n):
                c, j = divmod(n, NI)
                nT = onT[:, 2 * c + 1:2 * c + 3, 1, :]
                if n == 0:
                    pe.wait_ge(S["w_gu_ok"], 1)
                    pe.wait_ge(S["qheads_ok"], NB)
                if n == 1:
                    pe.wait_ge(S["ke_ok"], NB)
                if j == 0:
                    pe.wait_ge(S["onT_ok"], 2 * c + 3)
                if n >= 2:
                    pe.wait_ge(S["gates_ok"], n - 1)
                pe.matmul(gate_ps[n % 2][0:IW[j], :], w_gu[:, j * P:j * P + IW[j]], nT, start=True, stop=True)\
                    .then_inc(S["gate_pe"], 1)
                if n < 2:
                    pe.wait_ge(S["att_ok"], TB * (NB - 1) + n + 1)
                else:
                    pe.wait_ge(S["act_ok"], n - 1)
                pe.matmul(up_ps[n % 2][0:IW[j], :], w_gu[:, I + j * P:I + j * P + IW[j]], nT, start=True, stop=True)\
                    .then_inc(S["up_pe"], 1)

            def down(n):
                c, j = divmod(n, NI)
                pe.wait_ge(S["act_ok"], n + 1)
                if n == 0:
                    pe.wait_ge(down_w_in, 16 * NI)
                    pe.wait_ge(S["o_ok"], NB)
                if n == NI:
                    pe.wait_ge(S["onT_ok"], NB + 1)
                if j == 0 and c >= 2:
                    pe.wait_ge(S["t1_ok"], c - 1)
                for t in range(TC):
                    ins = pe.matmul(down_ps[c % 2][:, t * P:(t + 1) * P], act_T[0:IW[j], n % 3, t * P:(t + 1) * P],
                                    w_down[0:IW[j], j, :], start=(j == 0 and t == 0), stop=(j == NI - 1),
                                    skip_group_check=True)
                ins.then_inc(S["down_pe"], 1)

            def turn_y(c):
                pe.wait_ge(S["y_ok"], c + 1)
                if c >= 1:
                    pe.wait_ge(S["ylo_ok"], c)
                if c == 0:
                    pe.wait_ge(S["bin2T_ok"], 1)
                for t in range(TC):
                    ins = pe.transpose(yT_ps[:, t * P:(t + 1) * P], y[:, c * TC + t, :], ident[:, :])
                ins.then_inc(S["yT_pe"], 1)

            def hidden(n):
                c, j = divmod(n, NF)
                if n >= 3:
                    pe.wait_ge(S["hid_ok"], n - 2)
                pe.wait_ge(S["yhi_ok"], c + 1)
                if n == 0:
                    pe.wait_ge(S["x2_ok"], NB)
                elif n < 3:
                    pe.wait_ge(S["gates_ok"], NC * NI - 2 + n)
                w = sign1T[:, j * P:(j + 1) * P]
                pe.matmul(hid_ps[n % 3][:, :], w, y_hi[:, c % 2, :], start=True, stop=False)
                pe.wait_ge(S["ylo_ok"], c + 1)
                pe.matmul(hid_ps[n % 3][:, :], w, y_lo[:, c % 2, :], start=False, stop=True).then_inc(S["hid_pe"], 1)

            def ffn_out(n):
                c, j = divmod(n, NF)
                pe.wait_ge(S["hid_ok"], n + 1)
                if j == 0 and c >= 2:
                    pe.wait_ge(S["t2_ok"], c - 1)
                elif j == 0:
                    pe.wait_ge(S["act_ok"], NC * NI - 1 + c)
                if n == NF * (NC - 1):
                    pe.wait_ge(S["t1_ok"], NC)
                    pe.wait_ge(S["ylo_ok"], NC)
                for t in range(TC):
                    ins = pe.matmul(ffn_ps(c, t), hid[:, n % 3, t * P:(t + 1) * P],
                                    bin2T[:, j, :], start=(j == 0 and (t == 0 or c == NC - 1)), stop=(j == NF - 1),
                                    skip_group_check=True)
                    if n == NC * NF - 1 or t == TC - 1:
                        ins.then_inc(S["ffn_pe"], 1)

            for k in range(-3, NB):
                if 0 <= k < NB:
                    scores(k)
                    key_values(k)
                    if k == NB - 1:
                        turn_sign1()
                    outputs(k, 0)
                if 0 <= k + 1 < NB:
                    decay(k + 1)
                if 0 <= k < NB:
                    outputs(k, 1)
                if 0 <= k - 1:
                    turn_og_n(k - 1)
                if 0 <= k + 1 < NB:
                    turn_qk(k + 1)
                if 0 <= k + 3 < NB:
                    turn_x(k + 3)
                if k == NB - 1:
                    gate_up(0)
                if 0 <= k - 1:
                    project_out(k - 1)
                if 0 <= k + 2 < NB:
                    project(k + 2)
            gate_up(1)
            turn_og_n(NB - 1)
            turn_bin2()
            gate_up(2)
            project_out(NB - 1)
            down(0)
            gate_up(3)
            down(1)
            turn_og_n(NB)
            for n in range(4, NC * NI):
                down(n - 2)
                if n == NC * NI - 1:
                    turn_y(0)
                gate_up(n)
            down(NC * NI - 2)
            hidden(0)
            hidden(1)
            down(NC * NI - 1)
            turn_y(1)
            for n in range(2, NC * NF):
                hidden(n)
                if n % NF == 3 and n // NF + 2 < NC:
                    turn_y(n // NF + 2)
                ffn_out(n - 2)
            ffn_out(NC * NF - 2)
            ffn_out(NC * NF - 1)

        @block.scalar
        def _(act):
            nc.scalar.preload_act_table_set("natural_log_exp_and_others")
            act.dma_start(w_in[:, 2 * DK:2 * DK + DV], Wv).then_inc(attn_w_in, 16)
            act.dma_start(w_in[:, 2 * DK + DV:2 * DK + VG], Wg).then_inc(attn_w_in, 16)
            act.dma_start(anw[:, :], attn_norm_w.rearrange("(p a) -> p a", a=1)).then_inc(attn_w_in, 16)

            def root(ssq_sem, ln_sem, rs_sem, value, ssq, ln, rs, width):
                act.wait_ge(S[ssq_sem], value)
                act.activation(ln, ssq, ACT.Ln, bias=eps[:, :], scale=1.0 / width).then_inc(S[ln_sem], 1)
                act.wait_ge(S[ln_sem], value)
                act.activation(rs, ln, ACT.Exp, scale=-0.5).then_inc(S[rs_sem], 1)

            def root_x(b):
                root("xssq_ok", "xln_ok", "xrs_ok", b + 1, x_ssq[:, tiles(b)], x_ln[:, tiles(b)],
                     x_rs[:, tiles(b)], D)

            def copy_xT(b):
                act.wait_ge(S["xT_pe"], b + 1)
                act.activation(xT[:, b * BT:(b + 1) * BT], xT_ps, ACT.Copy).then_inc(S["xT_ok"], 1)

            def copy_vg(b):
                act.wait_ge(S["vg_pe"], b + 1)
                act.activation(vg[:, tiles(b), :], vg_ps, ACT.Copy).then_inc(S["vg_ok"], 1)

            def soft_z(b):
                act.wait_ge(S["zna_ok"], b + 1)
                if b >= 1:
                    act.wait_ge(S["zl_ok"], b)
                act.activation(z_e[:, :, :], z_na[:, :, :], ACT.Exp).then_inc(S["ze_ok"], 1)
                act.wait_ge(S["ze_ok"], b + 1)
                if b >= 1:
                    act.wait_ge(S["glog_ok"], b)
                act.activation(z_l[:, :, :], z_e[:, :, :], ACT.Ln, bias=1.0).then_inc(S["zl_ok"], 1)

            def soft_g(b):
                act.wait_ge(S["gna_ok"], b + 1)
                act.activation(g_e[:, :, :], g_na[:, :, :], ACT.Exp).then_inc(S["ge_ok"], 1)
                act.wait_ge(S["ge_ok"], b + 1)
                if b >= 1:
                    act.wait_ge(S["gls_ok"], b)
                act.activation(g_l[:, :, :], g_e[:, :, :], ACT.Ln, bias=1.0).then_inc(S["gl_ok"], 1)

            def sigmoid_g(b):
                act.wait_ge(S["gls_ok"], b + 1)
                if b >= 1:
                    act.wait_ge(S["gs_ok"], b)
                act.activation(g_sg[:, :, :], g_ls[:, :, :], ACT.Exp).then_inc(S["gsg_ok"], 1)

            def decays(b):
                act.wait_ge(S["carry_pe"], b + 1)
                if b >= 1:
                    act.wait_ge(S["qe_ok"], b)
                act.activation(grow[:, :], decay_ps, ACT.Exp).then_inc(S["grow_ok"], 1)
                if b >= 1:
                    act.wait_ge(S["ke_ok"], b)
                act.activation(fall[:, :], decay_ps, ACT.Exp, scale=-1.0).then_inc(S["fall_ok"], 1)
                if b >= 2:
                    act.wait_ge(S["kv_ok"], b - 1)
                act.activation(carry[:, b % 2, :], carry_ps, ACT.Exp).then_inc(S["carry_ok"], 1)

            def copy_qk(b):
                act.wait_ge(S["turn_pe"], b + 1)
                if b == 0:
                    act.wait_ge(S["pads_ok"], 1)
                if b >= 2:
                    act.wait_ge(S["a_pe"], TB * (b - 1))
                    act.wait_ge(S["o_pe"], b - 1)
                act.activation(kT[:, b % 2, :], bank_turn[:, 0:BT], ACT.Copy).then_inc(S["kT_ok"], 1)
                act.activation(qT1[:, b % 2, :], bank_turn[:, BT + P:2 * BT], ACT.Copy)
                for h in range(H):
                    rows = slice(h * HP, (h + 1) * HP)
                    ins = act.activation(qheads[rows, b % 2, :, h, :],
                                         bank_turn[rows, BT:2 * BT].rearrange("p (t c) -> p t c", t=TB), ACT.Copy)
                ins.then_inc(S["qheads_ok"], 1)

            def copy_o(b):
                act.wait_ge(S["o_pe"], b + 1)
                if b >= 2:
                    act.wait_ge(S["on_ok"], b - 1)
                    act.wait_ge(S["osq_ok"], b - 1)
                act.activation(o_sb[:, b % 2], o_ps, ACT.Copy).then_inc(S["o_ok"], 1)

            def root_o(b):
                root("ossq_ok", "oln_ok", "ors_ok", b + 1, o_ssq[:, tiles(b), :], o_ln[:, tiles(b), :],
                     o_rs[:, tiles(b), :], E)

            def copy_on(s):
                act.wait_ge(S["ogT_pe"], s + 1)
                a, z = (0 if s < NB else 1), (2 if s >= 1 else 1)
                act.activation(onT[:, s, a:z, :], bank_vg[:, a * BT:z * BT].rearrange("p (a c) -> p a c", c=BT),
                               ACT.Copy).then_inc(S["onT_ok"], 1)

            act.wait_ge(S["eps_ok"], 1)
            for k in range(-4, NB):
                if 0 <= k + 1 < NB:
                    copy_vg(k + 1)
                    soft_z(k + 1)
                if 0 <= k - 1 < NB:
                    root_o(k - 1)
                if 0 <= k + 1 < NB:
                    soft_g(k + 1)
                if 0 <= k + 4 < NB:
                    root_x(k + 4)
                if 0 <= k + 1 < NB:
                    decays(k + 1)
                if 0 <= k < NB:
                    copy_o(k)
                if 0 <= k - 1:
                    copy_on(k - 1)
                if 0 <= k + 1 < NB:
                    copy_qk(k + 1)
                    sigmoid_g(k + 1)
                if 0 <= k + 3 < NB:
                    copy_xT(k + 3)

            def silu(n):
                j = n % NI
                act.wait_ge(S["gate_pe"], n + 1)
                if n >= 2:
                    act.wait_ge(S["act_ok"], n - 1)
                act.activation(gate_s[0:IW[j], n % 2, :], gate_ps[n % 2][0:IW[j], :], ACT.Silu)\
                    .then_inc(S["gates_ok"], 1)

            def copy_sign1T():
                act.wait_ge(S["sign1T_ps"], 1)
                act.activation(sign1T[:, :], signs_ps[:, :], ACT.Copy).then_inc(S["sign1T_ok"], 1)

            def copy_bin2T():
                act.wait_ge(S["bin2T_ps"], 1)
                act.activation(bin2T[:, :, :], signs_ps[:, :].rearrange("p (j d) -> p j d", j=NF), ACT.Copy)\
                    .then_inc(S["bin2T_ok"], 1)

            def high_y(c):
                act.wait_ge(S["yT_pe"], c + 1)
                if c >= 2:
                    act.wait_ge(S["hid_pe"], NF * (c - 1))
                act.activation(y_hi[:, c % 2, :], yT_ps[:, :], ACT.Copy).then_inc(S["yhi_ok"], 1)

            def gelu(n):
                c, j = divmod(n, NF)
                act.wait_ge(S["hid_pe"], n + 1)
                if n >= 3:
                    act.wait_ge(S["ffn_pe"], n - 2)
                act.activation(hid[:, n % 3, :], hid_ps[n % 3][:, :], ACT.Gelu, bias=b1_col[:, j:j + 1],
                               scale=alpha1[:, j:j + 1]).then_inc(S["hid_ok"], 1)

            copy_sign1T()
            root_o(NB - 1)
            silu(0)
            silu(1)
            copy_on(NB - 1)
            copy_bin2T()
            silu(2)
            silu(3)
            copy_on(NB)
            for n in range(4, NC * NI):
                silu(n)
            high_y(0)
            act.wait_ge(S["alpha_ok"], 2)
            for n in range(NC * NF):
                gelu(n)
                if n == 0:
                    high_y(1)
                if n % NF == 3 and n // NF + 2 < NC:
                    high_y(n // NF + 2)

        @block.vector
        def _(dve):
            dve.memset(eps[:, :], RMS_EPS).then_inc(S["eps_ok"], 1)
            def squares_x(b):
                dve.wait_ge(x_in[b], 16)
                for t in range(TB):
                    i = b * TB + t
                    ins = dve.tensor_tensor_reduce(xh[:, i, :], xs[:, i, :], xs[:, i, :], 1.0, 0.0, ALU.mult,
                                                   ALU.add, x_ssq[:, i:i + 1])
                ins.then_inc(S["xssq_ok"], 1)

            def scale_x(b):
                dve.wait_ge(S["xrs_ok"], b + 1)
                for t in range(TB):
                    i = b * TB + t
                    ins = dve.tensor_scalar(xh[:, i, :], xs[:, i, :], x_rs[:, i:i + 1], None, ALU.mult)
                ins.then_inc(S["xh_ok"], 1)

            def z_start(b):
                dve.wait_ge(S["qkz_pe"], b + 1)
                bias = z_bias[:, :].unsqueeze(1).to_broadcast([P, TB, DK])
                if b >= 1:
                    dve.wait_ge(S["glog_ok"], b)
                dve.tensor_tensor(zb[:, :, :], qkz_ps[:, :, 2 * DK:QKZ], bias, ALU.add).then_inc(S["zb_ok"], 1)
                dve.wait_ge(S["zb_ok"], b + 1)
                if b >= 1:
                    dve.wait_ge(S["ze_ok"], b)
                dve.scalar_tensor_tensor(out=z_na[:, :, :], in0=zb[:, :, :], scalar=-1.0, in1=zb[:, :, :],
                                         op0=ALU.mult, op1=ALU.min).then_inc(S["zna_ok"], 1)

            def z_end(b):
                dve.wait_ge(S["zl_ok"], b + 1)
                if b == 0:
                    dve.wait_ge(S["pads_ok"], 1)
                if b >= 2:
                    dve.wait_ge(S["carry_pe"], b - 1)
                g4 = glog[:, b % 2].rearrange("p t (h d) -> p (t h) d", d=HP)[:, :, 0:HD]
                dve.scalar_tensor_tensor(out=g4, in0=zb[:, :, :].rearrange("p t (h d) -> p (t h) d", d=HD),
                                         scalar=0.0, in1=z_l[:, :, :].rearrange("p t (h d) -> p (t h) d", d=HD),
                                         op0=ALU.min, op1=ALU.subtract).then_inc(S["glog_ok"], 1)

            def g_start(b):
                dve.wait_ge(S["vg_ok"], b + 1)
                if b >= 1:
                    dve.wait_ge(S["ge_ok"], b)
                dve.scalar_tensor_tensor(out=g_na[:, :, :], in0=vg[:, tiles(b), DV:VG], scalar=-1.0,
                                         in1=vg[:, tiles(b), DV:VG], op0=ALU.mult, op1=ALU.min)\
                    .then_inc(S["gna_ok"], 1)

            def g_end(b):
                dve.wait_ge(S["gl_ok"], b + 1)
                if b >= 1:
                    dve.wait_ge(S["gsg_ok"], b)
                dve.scalar_tensor_tensor(out=g_ls[:, :, :], in0=vg[:, tiles(b), DV:VG], scalar=0.0,
                                         in1=g_l[:, :, :], op0=ALU.min, op1=ALU.subtract).then_inc(S["gls_ok"], 1)

            def scale_qk(b):
                if b >= 2:
                    dve.wait_ge(S["turn_pe"], b - 1)
                    dve.wait_ge(S["kv_pe"], b - 1)

                def heads(ap, width):
                    return ap.rearrange("p t (h d) -> p t h d", d=width)[:, :, :, 0:HD]
                dve.wait_ge(S["grow_ok"], b + 1)
                q_in = heads(qkz_ps[:, :, 0:DK], HD)
                k_in = heads(qkz_ps[:, :, DK:2 * DK], HD)
                g_in = grow[:, :].rearrange("p (t h d) -> p t h d", t=TB, h=H)
                f_in = fall[:, :].rearrange("p (t h d) -> p t h d", t=TB, h=H)
                dve.wait_ge(S["fall_ok"], b + 1)
                dve.tensor_tensor(heads(qe[:, b % 2], HP), q_in, g_in, ALU.mult).then_inc(S["qe_ok"], 1)
                dve.tensor_tensor(heads(ke[:, b % 2], HP), k_in, f_in, ALU.mult).then_inc(S["ke_ok"], 1)

            def mask(b, t):
                dve.wait_ge(S["a_pe"], TB * b + t + 1)
                if b == 0:
                    dve.wait_ge(S["pads_ok"], 2)
                if b >= 2:
                    dve.wait_ge(S["o_pe"], b - 1)
                dve.copy_predicated(att[:, b % 2, t, :], causal[:, :].bitcast(U32), bank_a[t][:, :])\
                    .then_inc(S["att_ok"], 1)

            def make_state(b):
                dve.wait_ge(S["kv_pe"], b + 1)
                dve.wait_ge(S["carry_ok"], b + 1)
                if b == 0:
                    dve.wait_ge(S["consts_ok"], 1)
                if b >= 2:
                    dve.wait_ge(S["o_pe"], b - 1)
                dve.scalar_tensor_tensor(out=state[:, b % 2, :], in0=kv_ps, scalar=carry[:, b % 2, 0:1],
                                         in1=same_head[:, :], op0=ALU.mult, op1=ALU.mult)\
                    .then_inc(S["kv_ok"], 1)

            def norm_o(b):
                dve.wait_ge(S["osq_ok"], b + 1)
                dve.tensor_reduce(o_ssq[:, tiles(b), :], o_sq[:, b % 2].rearrange("p t (h e) -> p t h e", e=E),
                                  AX.X, ALU.add).then_inc(S["ossq_ok"], 1)

            def gated(b):
                dve.wait_ge(S["ors_ok"], b + 1)
                rs = o_rs[:, tiles(b), :].unsqueeze(3).to_broadcast([P, TB, H, E])
                if b >= 1:
                    dve.wait_ge(S["og_ok"], b)
                dve.tensor_tensor(o_n[:, :, :].rearrange("p t (h e) -> p t h e", e=E),
                                  o_sb[:, b % 2].rearrange("p t (h e) -> p t h e", e=E), rs, ALU.mult)\
                    .then_inc(S["on_ok"], 1)
                dve.wait_ge(S["on_ok"], b + 1)
                dve.wait_ge(S["gs_ok"], b + 1)
                if b >= 2:
                    dve.wait_ge(S["ogT_pe"], b - 1)
                dve.tensor_tensor(og[:, b % 2], o_n[:, :, :], gs[:, b % 2], ALU.mult).then_inc(S["og_ok"], 1)

            def residual(b):
                dve.wait_ge(S["wo_pe"], b + 1)
                dve.tensor_tensor(x2[:, tiles(b), :], wo_ps, xs[:, tiles(b), :], ALU.add).then_inc(S["x2_ok"], 1)
                dve.wait_ge(S["x2_ok"], b + 1)
                for t in range(TB):
                    i = b * TB + t
                    ins = dve.tensor_tensor_reduce(y[:, i, :], x2[:, i, :], x2[:, i, :], 1.0, 0.0, ALU.mult,
                                                   ALU.add, x2_ssq[:, i:i + 1])
                ins.then_inc(S["x2ssq_ok"], 1)

            def scale_x2(b):
                dve.wait_ge(S["x2rs_ok"], b + 1)
                if b >= 2:
                    dve.wait_ge(S["ogT_pe"], b)
                for t in range(TB):
                    i = b * TB + t
                    ins = dve.tensor_scalar(n_sb[:, b % 2, t, :], x2[:, i, :], x2_rs[:, i:i + 1], None, ALU.mult)
                ins.then_inc(S["n_ok"], 1)

            squares_x(0)
            half = P // 2
            dve.memset(late_half[0:half, :], 0.0)
            dve.memset(late_half[half:P, :], 1.0 / GATE_NORMALIZER)
            dve.memset(early_half[0:half, :], 1.0 / GATE_NORMALIZER)
            dve.memset(early_half[half:P, :], 0.0)
            dve.memset(same_head[:, :], 0.0).then_inc(S["same_zero"], 1)
            dve.wait_ge(S["same_zero"], 1)
            for h in range(H):
                dve.memset(same_head[h * HP:(h + 1) * HP, h * E:(h + 1) * E], 1.0)
            dve.wait_ge(S["up_to_ok"], 1)
            dve.tensor_scalar(decay_sum[0:half, :], decay_sum[0:half, :], -1.0 / GATE_NORMALIZER, None, ALU.add)\
                .then_inc(S["consts_ok"], 1)
            scale_x(0)
            dve.wait_ge(gk_in, 48)
            dve.wait_ge(S["gk1T_ps"], 1)
            dve.tensor_copy(gk1T[:, :], bank_uw[0:R, 0:P]).then_inc(S["gk1T_ok"], 1)
            dve.wait_ge(attn_w_in, 80)
            dve.tensor_scalar(w_qkz[:, 0:DK], w_in[:, 0:DK], anw[:, 0:1], float(HD) ** -0.5, ALU.mult, ALU.mult)\
                .then_inc(S["w_attn_ok"], 1)
            dve.tensor_scalar(w_qkz[:, DK:2 * DK], w_in[:, DK:2 * DK], anw[:, 0:1], None, ALU.mult)
            dve.tensor_scalar(w_vg[:, :], w_in[:, 2 * DK:2 * DK + VG], anw[:, 0:1], None, ALU.mult)\
                .then_inc(S["w_attn_ok"], 1)
            dve.wait_ge(S["gkw_ps"], 1)
            dve.tensor_scalar(w_qkz[:, 2 * DK:QKZ], bank_uw[:, 0:DK], anw[:, 0:1], None, ALU.mult)\
                .then_inc(S["w_attn_ok"], 1)
            squares_x(1)
            scale_x(1)
            squares_x(2)

            def prepare_o():
                dve.wait_ge(wo_w_in, 16 * (1 + H))
                dve.tensor_scalar(w_o[:, :], wo_in[:, :], gnw[:, 0:1], None, ALU.mult).then_inc(S["w_o_ok"], 1)

            def prepare_mlp():
                dve.wait_ge(mlp_w_in, 48)
                dve.tensor_scalar(w_gu[:, :], gu_in[:, :], mnw[:, 0:1], None, ALU.mult).then_inc(S["w_gu_ok"], 1)

            def prepare_ffn():
                dve.wait_ge(ffn_w_in, 64)
                dve.tensor_scalar(neg1[:, :, :], w1_in[:, :, :], 0.0, None, ALU.is_lt).then_inc(S["half1_ok"], 1)
                dve.tensor_scalar(neg2[:, :], w2_in[:, :], 0.0, None, ALU.is_lt).then_inc(S["half2_ok"], 1)
                dve.wait_ge(S["half1_ok"], 1)
                dve.scalar_tensor_tensor(out=sign1[:, :, :], in0=w1_in[:, :, :], scalar=0.0, in1=neg1[:, :, :],
                                         op0=ALU.is_gt, op1=ALU.subtract).then_inc(S["sign1_ok"], 1)
                dve.wait_ge(S["half2_ok"], 1)
                dve.scalar_tensor_tensor(out=sign2[:, :], in0=w2_in[:, :], scalar=0.0, in1=neg2[:, :],
                                         op0=ALU.is_gt, op1=ALU.subtract).then_inc(S["sign2_ok"], 1)

            def prepare_alpha():
                dve.tensor_reduce(abs1[:, :], w1_in[:, :, :], AX.X, ALU.add, apply_absolute_value=True)
                dve.tensor_reduce(abs2[:, :], w2_in[:, :], AX.X, ALU.add, apply_absolute_value=True)\
                    .then_inc(S["abs_ok"], 1)
                dve.wait_ge(S["abs_ok"], 1)
                dve.tensor_scalar(alpha1[:, :], abs1[:, :], 1.0 / D, None, ALU.mult).then_inc(S["alpha_ok"], 1)
                dve.tensor_scalar(alpha2[:, :], abs2[:, :], 1.0 / HF, None, ALU.mult).then_inc(S["alpha_ok"], 1)
                dve.wait_ge(S["alpha_ok"], 2)
                dve.wait_ge(S["sign2_ok"], 1)
                dve.tensor_scalar(bin2[:, :], sign2[:, :], alpha2[:, 0:1], None, ALU.mult).then_inc(S["bin2_ok"], 1)

            for k in range(-2, NB):
                if 0 <= k + 1 < NB:
                    z_start(k + 1)
                    g_start(k + 1)
                if 0 <= k < NB:
                    mask(k, 0)
                if 0 <= k + 1 < NB:
                    z_end(k + 1)
                if 0 <= k < NB:
                    mask(k, 1)
                    make_state(k)
                if 0 <= k - 1 < NB:
                    gated(k - 1)
                if 0 <= k - 2 < NB - 1:
                    scale_x2(k - 2)
                if 0 <= k + 1 < NB:
                    scale_qk(k + 1)
                    g_end(k + 1)
                if 0 <= k + 4 < NB:
                    scale_x(k + 4)
                if 0 <= k - 1 < NB:
                    residual(k - 1)
                if 0 <= k < NB:
                    norm_o(k)
                if 0 <= k + 5 < NB:
                    squares_x(k + 5)
                if k == -1:
                    prepare_o()
                if k == 0:
                    prepare_mlp()
                if k == NB - 2:
                    prepare_ffn()
            prepare_alpha()

            def gated_up(n):
                j = n % NI
                dve.wait_ge(S["up_pe"], n + 1)
                dve.wait_ge(S["gates_ok"], n + 1)
                if n >= 3:
                    dve.wait_ge(S["down_pe"], n - 2)
                dve.tensor_tensor(act_T[0:IW[j], n % 3, :], up_ps[n % 2][0:IW[j], :], gate_s[0:IW[j], n % 2, :],
                                  ALU.mult).then_inc(S["act_ok"], 1)

            def moments(c, a, z, which, g, source, addend):
                q = c % 2
                dve.tensor_tensor(ln_in[:, q, a:z], source.rearrange("p (t d) -> p t d", d=D),
                                  addend[:, c * TC + a:c * TC + z, :], ALU.add).then_inc(S["t" + which], 1)
                dve.wait_ge(S["t" + which], g + 1)
                for t in range(a, z):
                    ins = dve.bn_stats(ln_st[:, q, t, :], ln_in[:, q, t, :])
                ins.then_inc(S["st" + which], 1)
                dve.wait_ge(S["st" + which], g + 1)
                for t in range(a, z):
                    ins = dve.bn_aggr(ln_mv[:, q, t, :], ln_st[:, q, t, :])
                ins.then_inc(S["mv" + which], 1)

            def normalize(c, a, z, which, g, dest, done):
                q = c % 2
                dve.wait_ge(S["rs" + which], g + 1)
                for t in range(a, z):
                    ins = dve.tensor_scalar(dest[:, c * TC + t, :], ln_in[:, q, t, :], ln_mv[:, q, t, 0:1],
                                            ln_rs[:, q, t:t + 1], ALU.subtract, ALU.mult)
                ins.then_inc(S[done], 1)

            def moments1(c):
                dve.wait_ge(S["xx2_ok"], (c + 1) * TC // TB)
                dve.wait_ge(S["down_pe"], NI * (c + 1))
                moments(c, 0, TC, "1_ok", c, down_ps[c % 2][:, :], xx2)

            def normalize1(c):
                normalize(c, 0, TC, "1_ok", c, y, "y_ok")

            def low_y(c):
                dve.wait_ge(S["yhi_ok"], c + 1)
                if c >= 2:
                    dve.wait_ge(S["hid_pe"], NF * (c - 1))
                dve.tensor_tensor(y_lo[:, c % 2, :], yT_ps[:, :], y_hi[:, c % 2, :].bitcast(F32), ALU.subtract)\
                    .then_inc(S["ylo_ok"], 1)

            def moments2(g):
                c, a, z = steps2[g]
                dve.wait_ge(S["yb_ok"], c + 1)
                dve.wait_ge(S["ffn_pe"], NF * (c + 1) if c < NC - 1 else NF * NC - 1 + z)
                moments(c, a, z, "2_ok", g, ffn_ps(c, a) if z == a + 1 else bank_a[c % 2][:, :], yb)

            def normalize2(g):
                c, a, z = steps2[g]
                normalize(c, a, z, "2_ok", g, y_out, "yout_ok")

            scale_x2(NB - 2)
            gated(NB - 1)
            gated_up(0)
            gated_up(1)
            residual(NB - 1)
            gated_up(2)
            scale_x2(NB - 1)
            for n in range(3, NC * NI):
                gated_up(n)
                if n % NI == 1:
                    moments1(n // NI - 1)
                if n % NI == 2:
                    normalize1(n // NI - 1)
            low_y(0)
            moments1(NC - 1)
            low_y(1)
            normalize1(NC - 1)
            for g in range(len(steps2)):
                if g + 2 < NC:
                    low_y(g + 2)
                moments2(g)
                if g < NC - 1:
                    normalize2(g)
                elif g >= NC:
                    normalize2(g - 1)
            normalize2(len(steps2) - 1)


_INS = ['L0_attn_hidden_states', 'L0_attn_attn_norm_w', 'L0_attn_Wq', 'L0_attn_Wk', 'L0_attn_Wv', 'L0_attn_Wg',
        'L0_attn_Wgk1', 'L0_attn_Wgk2', 'L0_attn_bgk2', 'L0_attn_gnorm_w', 'L0_attn_Wo', 'L0_attn_mlp_norm_w',
        'L0_attn_W_gate', 'L0_attn_W_up', 'L0_attn_W_down', 'L0_ffn_w1', 'L0_ffn_b1', 'L0_ffn_w2', 'L0_ffn_b2']


def kernel(**inputs):
    import numpy as np
    import concourse.bacc as bacc
    from concourse.bass_utils import run_bass_kernel_spmd

    nc = bacc.Bacc("TRN2", target_bir_lowering=False, num_devices=1)
    arrays, args = {}, []
    for name in _INS:
        a = np.ascontiguousarray(inputs[name])
        arrays[f"in_{name}_dram"] = a
        args.append(nc.dram_tensor(f"in_{name}_dram", a.shape, mybir.dt.from_np(a.dtype), kind="ExternalInput").ap())
    shape = inputs['L0_attn_hidden_states'].shape
    args.append(nc.dram_tensor("out_dram", shape, F32, kind="ExternalOutput").ap())
    gla_block_and_binary_ffn(nc, *args)
    result = run_bass_kernel_spmd(nc, [arrays], core_ids=[0])
    return result.results[0]["out_dram"]
```

```python
from contextlib import ExitStack

import concourse.bass as bass
from concourse import mybir

F32 = mybir.dt.float32
F32R = mybir.dt.float32r
U32 = mybir.dt.uint32
ALU = mybir.AluOpType
ACT = mybir.ActivationFunctionType
AX = mybir.AxisListType

P = 128
RMS_EPS = 1e-6
LN_EPS = 1e-5
GATE_NORMALIZER = 16.0
BATCH_TILES = 2
CHUNK_TILES = 4


def gla_block_and_binary_ffn(nc, x, attn_norm_w, Wq, Wk, Wv, Wg, Wgk1, Wgk2, bgk2, gnorm_w, Wo,
                             mlp_norm_w, W_gate, W_up, W_down, w1, b1, w2, b2, out):
    B, T, D = x.shape
    DK = Wq.shape[1]
    DV = Wv.shape[1]
    R = Wgk1.shape[1]
    E = gnorm_w.shape[0]
    H = DV // E
    HD = DK // H
    HP = P // H
    I = W_gate.shape[1]
    HF = w1.shape[0]
    NB, TB, TC = B, BATCH_TILES, CHUNK_TILES
    NT = B * T // P
    NC = NT // TC
    CH = TC * P
    BT = TB * P
    NI = -(-I // P)
    NF = HF // P
    IW = [min(P, I - j * P) for j in range(NI)]
    QKZ, VG = 2 * DK + DK, 2 * DV
    assert T == BT and D == P and DV == P and H * HP == P and HD <= HP and E == HP
    assert TB * QKZ <= 512 and TB * VG <= 512 and TB * H * P <= 1024 and CH == 512

    with ExitStack() as ctx:
        def sb(name, shape, dt=F32):
            return ctx.enter_context(nc.sbuf_tensor(name, shape, dt))

        def bank(name):
            return ctx.enter_context(nc.psum_tensor(name, [P, 512], F32))

        def sem(name):
            return ctx.enter_context(nc.semaphore(name))

        bank_qkz, bank_vg, bank_turn = bank("bank_qkz"), bank("bank_vg"), bank("bank_turn")
        bank_a = [bank("bank_a0"), bank("bank_a1")]
        bank_o, bank_dx, bank_uw = bank("bank_o"), bank("bank_dx"), bank("bank_uw")
        qkz_ps = bank_qkz[:, 0:TB * QKZ].rearrange("p (t n) -> p t n", t=TB)
        vg_ps = bank_vg[:, :].rearrange("p (t n) -> p t n", t=TB)
        o_ps = bank_o[:, 0:TB * DV].rearrange("p (t n) -> p t n", t=TB)
        xT_ps = bank_dx[:, 0:BT]
        decay_ps = bank_dx[:, BT:BT + TB * DK]
        carry_ps = bank_dx[:, BT + TB * DK:BT + TB * DK + 2]
        kv_ps = bank_uw[:, 0:DV]
        wo_ps = bank_uw[:, DV:DV + TB * D].rearrange("p (t n) -> p t n", t=TB)
        gate_ps = [bank_qkz, bank_turn]
        up_ps = bank_a
        down_ps = [bank_o, bank_vg]
        signs_ps = yT_ps = bank_dx
        hid_ps = [bank_uw, bank_qkz, bank_turn]

        def ffn_ps(c, t):
            if c < NC - 1:
                return bank_a[c % 2][:, t * P:(t + 1) * P]
            return [bank_a[1], bank_o, bank_vg, bank_dx][t][:, 0:P]

        ident = sb("ident", [P, P])
        causal = sb("causal", [P, H * P])
        decay_sum = sb("decay_sum", [P, P])
        late_half = sb("late_half", [P, 2])
        early_half = sb("early_half", [P, 2])
        same_head = sb("same_head", [P, DV])
        eps = sb("eps", [P, 1])
        busy = sb("busy", [P, P])
        minus_half = sb("minus_half", [P, TC])
        w_in = sb("w_in", [P, 2 * DK + 2 * DV])
        anw = sb("anw", [P, 1])
        gk1_in = sb("gk1_in", [P, R])
        gk2_in = sb("gk2_in", [R, DK])
        z_bias = sb("z_bias", [P, DK])
        wo_in = sb("wo_in", [P, D])
        gnw = sb("gnw", [P, 1])
        mnw = sb("mnw", [P, 1])
        gu_in = sb("gu_in", [P, 2 * I])
        w1_in = sb("w1_in", [P, NF, D])
        w2_in = sb("w2_in", [P, HF])
        b1_col = sb("b1_col", [P, NF])
        b2_row = sb("b2_row", [P, D])
        gk1T = sb("gk1T", [R, P])
        w_qkz = sb("w_qkz", [P, QKZ])
        w_vg = sb("w_vg", [P, VG])
        w_o = sb("w_o", [P, D])
        w_gu = sb("w_gu", [P, 2 * I])
        w_down = sb("w_down", [P, NI, D])
        neg1 = sb("neg1", [P, NF, D])
        pos1 = sb("pos1", [P, NF, D])
        sign1 = sb("sign1", [P, NF, D])
        neg2 = sb("neg2", [P, HF])
        pos2 = sb("pos2", [P, HF])
        sign2 = sb("sign2", [P, HF])
        bin2 = sb("bin2", [P, HF])
        abs1 = sb("abs1", [P, NF])
        alpha1 = sb("alpha1", [P, NF])
        abs2 = sb("abs2", [P, 1])
        alpha2 = sb("alpha2", [P, 1])
        sign1T = sb("sign1T", [P, HF], F32R)
        bin2T = sb("bin2T", [P, NF, D])
        xs = sb("xs", [P, NT, D])
        x_ssq = sb("x_ssq", [P, NT])
        x_ln = sb("x_ln", [P, NT])
        x_rs = sb("x_rs", [P, NT])
        xh = sb("xh", [P, NT, D])
        xT = sb("xT", [P, NT * P])
        zb = sb("zb", [P, TB, DK])
        z_na = sb("z_na", [P, TB, DK])
        z_e = sb("z_e", [P, TB, DK])
        z_l = sb("z_l", [P, TB, DK])
        glog = sb("glog", [P, 2, TB, P])
        vg = sb("vg", [P, NT, VG])
        g_na = sb("g_na", [P, TB, DV])
        g_e = sb("g_e", [P, TB, DV])
        g_l = sb("g_l", [P, TB, DV])
        g_ls = sb("g_ls", [P, TB, DV])
        g_sg = sb("g_sg", [P, TB, DV])
        gs = sb("gs", [P, 2, TB, DV])
        grow = sb("grow", [P, TB * DK])
        fall = sb("fall", [P, TB * DK])
        carry = sb("carry", [P, 2, 2])
        qe = sb("qe", [P, 2, TB, P])
        ke = sb("ke", [P, 2, TB, P])
        kT = sb("kT", [P, 2, BT])
        qT1 = sb("qT1", [P, 2, P])
        qheads = sb("qheads", [P, 2, TB, H, P])
        att = sb("att", [P, 2, TB, H * P])
        state = sb("state", [P, 2, DV])
        o_sb = sb("o_sb", [P, 2, TB, DV])
        o_sq = sb("o_sq", [P, 2, TB, DV])
        o_ssq = sb("o_ssq", [P, NT, H])
        o_ln = sb("o_ln", [P, NT, H])
        o_rs = sb("o_rs", [P, NT, H])
        o_n = sb("o_n", [P, TB, DV])
        og = sb("og", [P, 2, TB, DV])
        onT = sb("onT", [P, NB + 1, 2, BT])
        x2 = sb("x2", [P, NT, D])
        x2_ssq = sb("x2_ssq", [P, NT])
        x2_ve = sb("x2_ve", [P, NT])
        x2_rs = sb("x2_rs", [P, NT])
        n_sb = sb("n_sb", [P, 2, TB, D])
        xx2 = sb("xx2", [P, NT, D])
        gate_s = sb("gate_s", [P, 2, CH])
        act_T = sb("act_T", [P, 3, CH])
        ln_in = sb("ln_in", [P, 2, TC, D])
        ln_st = sb("ln_st", [P, 2, TC, 6])
        ln_mv = sb("ln_mv", [P, 2, TC, 2])
        ln_ve = sb("ln_ve", [P, 2, TC])
        ln_rs = sb("ln_rs", [P, 2, TC])
        ln_nm = sb("ln_nm", [P, TC])
        ln_nb = sb("ln_nb", [P, TC])
        y = sb("y", [P, NT, D])
        yb = sb("yb", [P, NT, D])
        y_hi = sb("y_hi", [P, 2, CH], F32R)
        y_lo = sb("y_lo", [P, 2, CH], F32R)
        hid = sb("hid", [P, 4, CH])
        y_out = xh

        x_in = [sem(f"x_in{b}") for b in range(NB)]
        attn_w_in, gk1_w_in, gk2_w_in = sem("attn_w_in"), sem("gk1_w_in"), sem("gk2_w_in")
        z_bias_in, wo_w_in, mlp_w_in = sem("z_bias_in"), sem("wo_w_in"), sem("mlp_w_in")
        down_w_in, ffn_w_in, out_done = sem("down_w_in"), sem("ffn_w_in"), sem("out_done")
        S = {}
        for name in (
            "eps_ok",
            "ident_ok",
            "consts_zero",
            "up_to_ok",
            "same_zero",
            "consts_ok",
            "pads_ok",
            "gk1T_ps",
            "gk1T_ok",
            "gkw_ps",
            "w_qkz_ok",
            "w_vg_ok",
            "warm_ok",
            "w_o_ok",
            "w_gu_ok",
            "half1_ok",
            "sign1_ok",
            "half2_ok",
            "sign2_ok",
            "abs_ok",
            "alpha_ok",
            "bin2_ok",
            "sign1T_ps",
            "sign1T_ok",
            "bin2T_ps",
            "bin2T_ok",
            "half_ok",
        ):
            S[name] = sem(name)
        for name in (
            "xssq_ok",
            "xln_ok",
            "xrs_ok",
            "xh_ok",
            "xT_pe",
            "xT_ok",
            "qkz_pe",
            "vg_pe",
            "vg_ok",
            "zb_ok",
            "zna_ok",
            "ze_ok",
            "zl_ok",
            "glog_ok",
            "gna_ok",
            "ge_ok",
            "gl_ok",
            "gls_ok",
            "gsg_ok",
            "gs_ok",
            "carry_pe",
            "grow_ok",
            "fall_ok",
            "carry_ok",
            "qe_ok",
            "ke_ok",
            "turn_pe",
            "kT_ok",
            "qheads_ok",
            "qT1_ok",
            "a_pe",
            "att_ok",
            "kv_pe",
            "kv_ok",
            "o_pe",
            "o_ok",
            "osq_ok",
            "ossq_ok",
            "oln_ok",
            "ors_ok",
            "on_ok",
            "og_ok",
            "ogT_pe",
            "onT_ok",
            "wo_pe",
            "x2_ok",
            "x2ssq_ok",
            "x2ve_ok",
            "x2rs_ok",
            "n_ok",
            "xx2_ok",
        ):
            S[name] = sem(name)
        for name in (
            "gate_pe",
            "up_pe",
            "gates_ok",
            "act_ok",
            "down_pe",
            "t1_ok",
            "st1_ok",
            "mv1_ok",
            "ve1_ok",
            "rs1_ok",
            "y_ok",
            "yb_ok",
        ):
            S[name] = sem(name)
        for name in (
            "yT_pe",
            "yhi_ok",
            "ylo_ok",
            "hid_pe",
            "hid_ok",
            "ffn_pe",
            "t2_ok",
            "st2_ok",
            "mv2_ok",
            "ve2_ok",
            "rs2_ok",
            "nm_ok",
            "nb_ok",
            "yout_ok",
            "yout_act",
        ):
            S[name] = sem(name)

        def tiles(b):
            return slice(b * TB, (b + 1) * TB)

        def ctiles(c):
            return slice(c * TC, (c + 1) * TC)

        steps2 = [(c, 0, TC) for c in range(NC - 1)] + [(NC - 1, t, t + 1) for t in range(TC)]

        block = ctx.enter_context(nc.Block())

        @block.sync
        def _(sp):
            xv = x.rearrange("b (t p) d -> p (b t) d", p=P)
            ov = out.rearrange("b (t p) d -> p (b t) d", p=P)
            sp.dma_start(xs[:, tiles(0), :], xv[:, tiles(0), :]).then_inc(x_in[0], 16)
            sp.dma_start(w_in[:, 0:DK], Wq).then_inc(attn_w_in, 16)
            sp.dma_start(w_in[:, DK:2 * DK], Wk).then_inc(attn_w_in, 16)
            sp.dma_start(xs[:, tiles(1), :], xv[:, tiles(1), :]).then_inc(x_in[1], 16)
            sp.dma_start(z_bias[:, :], bgk2.partition_broadcast(P)).then_inc(z_bias_in, 16)
            sp.dma_start(xs[:, tiles(2), :], xv[:, tiles(2), :]).then_inc(x_in[2], 16)
            sp.dma_start(wo_in[:, :], Wo).then_inc(wo_w_in, 16)
            for h in range(H):
                sp.dma_start(gnw[h * E:(h + 1) * E, :], gnorm_w.rearrange("(e a) -> e a", a=1)).then_inc(wo_w_in, 16)
            for b in range(3, NB):
                sp.dma_start(xs[:, tiles(b), :], xv[:, tiles(b), :]).then_inc(x_in[b], 16)
            sp.dma_start(gu_in[:, 0:I], W_gate).then_inc(mlp_w_in, 16)
            sp.dma_start(gu_in[:, I:2 * I], W_up).then_inc(mlp_w_in, 16)
            sp.dma_start(mnw[:, :], mlp_norm_w.rearrange("(p a) -> p a", a=1)).then_inc(mlp_w_in, 16)
            sp.dma_start(w1_in[:, :, :], w1.rearrange("(p j) d -> p j d", p=P)).then_inc(ffn_w_in, 16)
            sp.dma_start(w2_in[:, :], w2).then_inc(ffn_w_in, 16)
            sp.dma_start(b1_col[:, :], b1.rearrange("(p j) -> p j", p=P)).then_inc(ffn_w_in, 16)
            sp.dma_start(b2_row[:, :], b2.partition_broadcast(P)).then_inc(ffn_w_in, 16)
            for j in range(NI):
                sp.dma_start(w_down[0:IW[j], j, :], W_down[j * P:j * P + IW[j], :]).then_inc(down_w_in, 16)
            for g, (c, a, z) in enumerate(steps2):
                i, e = c * TC + a, c * TC + z
                if c == NC - 2:
                    sp.wait_ge(S["yout_act"], 1)
                else:
                    sp.wait_ge(S["yout_ok"], g + 1 - (c > NC - 2))
                sp.dma_start(ov[:, i:e, :], y_out[:, i:e, :]).then_inc(out_done, 16)
            sp.wait_ge(out_done, 16 * len(steps2))

        @block.gpsimd
        def _(pool):
            pool.memset(ident[:, :], 0.0).then_inc(S["consts_zero"], 1)
            pool.wait_ge(S["consts_zero"], 1)
            pool.affine_select(out=ident[:, :], in_=ident[:, :], compare_op=ALU.not_equal, fill=1.0, base=0,
                               pattern=[[-1, P]], channel_multiplier=1).then_inc(S["ident_ok"], 1)
            pool.dma_start(gk1_in[:, :], Wgk1).then_inc(gk1_w_in, 16)
            pool.dma_start(gk2_in[:, :], Wgk2).then_inc(gk2_w_in, 16)
            pool.memset(decay_sum[:, :], 0.0)
            pool.memset(causal[:, :], 0.0).then_inc(S["consts_zero"], 1)
            pool.wait_ge(S["consts_zero"], 2)
            pool.affine_select(out=decay_sum[:, :], in_=decay_sum[:, :], compare_op=ALU.is_gt,
                               fill=1.0 / GATE_NORMALIZER, base=0, pattern=[[-1, P]], channel_multiplier=1)\
                .then_inc(S["up_to_ok"], 1)
            pool.memset(glog[:, :, :, :], 0.0)
            pool.memset(qe[:, :, :, :], 0.0)
            pool.memset(ke[:, :, :, :], 0.0)
            pool.memset(qheads[:, :, :, :, :], 0.0).then_inc(S["pads_ok"], 1)
            pool.affine_select(out=causal[:, :], in_=causal[:, :], compare_op=ALU.is_gt, fill=1.0, base=0,
                               pattern=[[0, H], [-1, P]], channel_multiplier=1)
            pool.memset(att[:, :, :, :], 0.0).then_inc(S["pads_ok"], 1)
            pool.memset(minus_half[:, :], -0.5).then_inc(S["half_ok"], 1)

            def gate_product(b):
                pool.wait_ge(S["gsg_ok"], b + 1)
                pool.wait_ge(S["vg_ok"], b + 1)
                if b >= 2:
                    pool.wait_ge(S["og_ok"], b - 1)
                pool.tensor_tensor(gs[:, b % 2], vg[:, tiles(b), DV:VG], g_sg[:, :, :], ALU.mult)\
                    .then_inc(S["gs_ok"], 1)

            def o_squares(b):
                pool.wait_ge(S["o_ok"], b + 1)
                if b >= 2:
                    pool.wait_ge(S["ossq_ok"], b - 1)
                pool.tensor_tensor(o_sq[:, b % 2], o_sb[:, b % 2], o_sb[:, b % 2], ALU.mult).then_inc(S["osq_ok"], 1)

            def x_plus_x2(b):
                pool.wait_ge(S["x2_ok"], b + 1)
                pool.tensor_tensor(xx2[:, tiles(b), :], xs[:, tiles(b), :], x2[:, tiles(b), :], ALU.add)\
                    .then_inc(S["xx2_ok"], 1)

            def root_x2(b):
                pool.wait_ge(S["x2ssq_ok"], b + 1)
                pool.tensor_scalar(x2_ve[:, tiles(b)], x2_ssq[:, tiles(b)], 1.0 / D, RMS_EPS, ALU.mult, ALU.add)\
                    .then_inc(S["x2ve_ok"], 1)
                pool.wait_ge(S["x2ve_ok"], b + 1)
                pool.tensor_tensor(x2_rs[:, tiles(b)], x2_ve[:, tiles(b)], minus_half[:, 0:TB], ALU.pow)\
                    .then_inc(S["x2rs_ok"], 1)

            pool.wait_ge(S["half_ok"], 1)
            for k in range(-1, NB + 1):
                if 0 <= k < NB:
                    o_squares(k)
                if k >= 1:
                    root_x2(k - 1)
                if k + 1 < NB:
                    gate_product(k + 1)
                if k >= 1:
                    x_plus_x2(k - 1)
                if k == NB - 7:
                    pool.wait_ge(ffn_w_in, 64)
                    pool.tensor_scalar(neg1[:, :, :], w1_in[:, :, :], 0.0, None, ALU.is_lt).then_inc(S["half1_ok"], 1)
                if k == NB - 6:
                    pool.tensor_scalar(pos1[:, :, :], w1_in[:, :, :], 0.0, None, ALU.is_gt).then_inc(S["half1_ok"], 1)
                if k == NB - 5:
                    pool.wait_ge(S["half1_ok"], 2)
                    pool.tensor_tensor(sign1[:, :, :], pos1[:, :, :], neg1[:, :, :], ALU.subtract)\
                        .then_inc(S["sign1_ok"], 1)
                if k == NB - 4:
                    pool.tensor_scalar(neg2[:, :], w2_in[:, :], 0.0, None, ALU.is_lt).then_inc(S["half2_ok"], 1)
                if k == NB - 3:
                    pool.tensor_scalar(pos2[:, :], w2_in[:, :], 0.0, None, ALU.is_gt).then_inc(S["half2_ok"], 1)
                if k == NB - 2:
                    pool.wait_ge(S["half2_ok"], 2)
                    pool.tensor_tensor(sign2[:, :], pos2[:, :], neg2[:, :], ALU.subtract).then_inc(S["sign2_ok"], 1)

            def root_var(mv, ve, rs, which, g):
                pool.wait_ge(S["mv" + which], g + 1)
                pool.tensor_scalar(ve, mv, LN_EPS, 1.0, ALU.add, ALU.mult).then_inc(S["ve" + which], 1)
                pool.wait_ge(S["ve" + which], g + 1)
                pool.tensor_tensor(rs, ve, minus_half[:, 0:ve.shape[1]], ALU.pow).then_inc(S["rs" + which], 1)

            pool.wait_ge(ffn_w_in, 64)
            for c in range(NC):
                root_var(ln_mv[:, c % 2, :, 1], ln_ve[:, c % 2], ln_rs[:, c % 2], "1_ok", c)
                pool.wait_ge(S["y_ok"], c + 1)
                for t in range(TC):
                    i = c * TC + t
                    ins = pool.tensor_tensor(yb[:, i, :], y[:, i, :], b2_row[:, :], ALU.add)
                ins.then_inc(S["yb_ok"], 1)
            for g, (c, a, z) in enumerate(steps2):
                if c == NC - 2:
                    pool.wait_ge(S["mv2_ok"], g + 1)
                    pool.tensor_scalar(ln_nm[:, :], ln_mv[:, c % 2, :, 0], -1.0, 0.0, ALU.mult, ALU.add)\
                        .then_inc(S["nm_ok"], 1)
                root_var(ln_mv[:, c % 2, a:z, 1], ln_ve[:, c % 2, a:z], ln_rs[:, c % 2, a:z], "2_ok", g)
                if c == NC - 2:
                    pool.wait_ge(S["nm_ok"], 1)
                    pool.wait_ge(S["rs2_ok"], g + 1)
                    pool.tensor_tensor(ln_nb[:, :], ln_nm[:, :], ln_rs[:, c % 2, :], ALU.mult)\
                        .then_inc(S["nb_ok"], 1)

        @block.tensor
        def _(pe):
            def turn_x(b):
                pe.wait_ge(S["xh_ok"], b + 1)
                if b >= 1:
                    pe.wait_ge(S["xT_ok"], b)
                if b >= 2:
                    pe.wait_ge(S["carry_ok"], b - 1)
                for t in range(TB):
                    ins = pe.transpose(xT_ps[:, t * P:(t + 1) * P], xh[:, b * TB + t, :], ident[:, :])
                ins.then_inc(S["xT_pe"], 1)

            def project_qkz(b):
                if b == 0:
                    pe.wait_ge(S["w_qkz_ok"], 2)
                pe.wait_ge(S["xT_ok"], b + 1)
                if b >= 1:
                    pe.wait_ge(S["ke_ok"], b)
                for t in range(TB):
                    i = b * TB + t
                    ins = pe.matmul(qkz_ps[:, t, :], xT[:, i * P:(i + 1) * P], w_qkz[:, :], start=True, stop=True)
                ins.then_inc(S["qkz_pe"], 1)

            def project_vg(b):
                if b == 0:
                    pe.wait_ge(S["w_vg_ok"], 1)
                pe.wait_ge(S["xT_ok"], b + 1)
                if b >= 1:
                    pe.wait_ge(S["vg_ok"], b)
                if b >= 3:
                    pe.wait_ge(S["onT_ok"], b - 2)
                for t in range(TB):
                    i = b * TB + t
                    ins = pe.matmul(vg_ps[:, t, :], xT[:, i * P:(i + 1) * P], w_vg[:, :], start=True, stop=True)
                ins.then_inc(S["vg_pe"], 1)

            def decay(b):
                pe.wait_ge(S["glog_ok"], b + 1)
                if b >= 1:
                    pe.wait_ge(S["carry_ok"], b)
                pe.wait_ge(S["xT_ok"], min(b + 2, NB))
                g4 = glog[:, b % 2].rearrange("p t (h d) -> p (t h) d", d=HP)[:, :, 0:HD]
                pe.matmul(decay_ps, decay_sum[:, :], g4, start=True, stop=True)
                pe.matmul(carry_ps, glog[:, b % 2, 0, :], late_half[:, :], start=True, stop=False)
                pe.matmul(carry_ps, glog[:, b % 2, 1, :], early_half[:, :], start=False, stop=True)\
                    .then_inc(S["carry_pe"], 1)

            def turn_qk(b):
                pe.wait_ge(S["qe_ok"], b + 1)
                pe.wait_ge(S["ke_ok"], b + 1)
                if b >= 1:
                    pe.wait_ge(S["qT1_ok"], b)
                for t in range(TB):
                    pe.transpose(bank_turn[:, t * P:(t + 1) * P], ke[:, b % 2, t, :], ident[:, :])
                for t in range(TB):
                    ins = pe.transpose(bank_turn[:, BT + t * P:BT + (t + 1) * P], qe[:, b % 2, t, :], ident[:, :])
                ins.then_inc(S["turn_pe"], 1)

            def scores(b):
                pe.wait_ge(S["kT_ok"], b + 1)
                for t in range(TB):
                    pe.wait_ge(S["qheads_ok"], TB * b + t + 1)
                    if b >= 1:
                        pe.wait_ge(S["att_ok"], TB * (b - 1) + t + 1)
                    pe.matmul(bank_a[t][:, :], kT[:, b % 2, t * P:(t + 1) * P],
                              qheads[:, b % 2, t].rearrange("p h c -> p (h c)"),
                              start=True, stop=True).then_inc(S["a_pe"], 1)

            def key_values(b):
                if b >= 2:
                    pe.wait_ge(S["x2_ok"], b - 1)
                pe.matmul(kv_ps, ke[:, b % 2, 0, :], vg[:, b * TB, 0:DV], start=True, stop=True)\
                    .then_inc(S["kv_pe"], 1)

            def outputs(b, t):
                pe.wait_ge(S["att_ok"], TB * b + t + 1)
                if t == 0 and b >= 1:
                    pe.wait_ge(S["o_ok"], b)
                for h in range(H):
                    pe.matmul(o_ps[:, t, h * E:(h + 1) * E], att[:, b % 2, t, h * P:(h + 1) * P],
                              vg[:, b * TB + t, h * E:(h + 1) * E], start=(t == 0 and h == 0), stop=False,
                              skip_group_check=True)
                if t == 1:
                    pe.wait_ge(S["kv_ok"], b + 1)
                    pe.wait_ge(S["qT1_ok"], b + 1)
                    pe.matmul(o_ps[:, 1, :], qT1[:, b % 2, :], state[:, b % 2, :], start=False, stop=True,
                              skip_group_check=True).then_inc(S["o_pe"], 1)

            def turn_og_n(s):
                pe.wait_ge(S["og_ok"], s + 1)
                if s >= 1:
                    if s < NB - 1:
                        pe.wait_ge(S["n_ok"], s)
                    pe.wait_ge(S["onT_ok"], s)
                pe.wait_ge(S["vg_ok"], min(s + 2, NB))
                for t in range(TB):
                    ins = pe.transpose(bank_vg[:, t * P:(t + 1) * P], og[:, s % 2, t, :], ident[:, :])
                for t in range(TB):
                    if 1 <= s < NB - 1:
                        ins = pe.transpose(bank_vg[:, BT + t * P:BT + (t + 1) * P], n_sb[:, (s - 1) % 2, t, :],
                                           ident[:, :])
                ins.then_inc(S["ogT_pe"], 1)

            def turn_last_n():
                pe.wait_ge(S["n_ok"], NB)
                pe.wait_ge(S["onT_ok"], NB)
                for i in range(2 * TB):
                    ins = pe.transpose(bank_vg[:, i * P:(i + 1) * P], n_sb[:, (NB - 2 + i // TB) % 2, i % TB, :],
                                       ident[:, :])
                ins.then_inc(S["ogT_pe"], 1)

            def project_out(b):
                if b == 0:
                    pe.wait_ge(S["w_o_ok"], 1)
                pe.wait_ge(S["onT_ok"], b + 1)
                pe.wait_ge(S["kv_ok"], min(b + 2, NB))
                if b >= 1:
                    pe.wait_ge(S["x2_ok"], b)
                for t in range(TB):
                    ins = pe.matmul(wo_ps[:, t, :], onT[:, b, 0, t * P:(t + 1) * P], w_o[:, :], start=True, stop=True)
                ins.then_inc(S["wo_pe"], 1)

            def turn_sign1():
                pe.wait_ge(S["sign1_ok"], 1)
                pe.wait_ge(S["xT_ok"], NB)
                pe.wait_ge(S["carry_ok"], NB)
                for j in range(NF):
                    ins = pe.transpose(signs_ps[:, j * P:(j + 1) * P], sign1[:, j, :], ident[:, :])
                ins.then_inc(S["sign1T_ps"], 1)

            def turn_bin2():
                pe.wait_ge(S["bin2_ok"], 1)
                pe.wait_ge(S["sign1T_ok"], 1)
                for j in range(NF):
                    ins = pe.transpose(signs_ps[:, j * P:(j + 1) * P], bin2[:, j:HF:NF], ident[:, :])
                ins.then_inc(S["bin2T_ps"], 1)

            def gate(n):
                c, j = divmod(n, NI)
                if n == 0:
                    pe.wait_ge(S["w_gu_ok"], 1)
                    pe.wait_ge(S["ke_ok"], NB)
                if n == 1:
                    pe.wait_ge(S["qT1_ok"], NB)
                if j == 0:
                    pe.wait_ge(S["onT_ok"], 2 * c + 3)
                if n >= 2:
                    pe.wait_ge(S["gates_ok"], n - 1)
                pe.matmul(gate_ps[n % 2][0:IW[j], :], w_gu[:, j * P:j * P + IW[j]],
                          onT[:, 2 * c + 1:2 * c + 3, 1, :], start=True, stop=True).then_inc(S["gate_pe"], 1)

            def up(n):
                c, j = divmod(n, NI)
                if n < 2:
                    pe.wait_ge(S["att_ok"], TB * (NB - 1) + n + 1)
                else:
                    pe.wait_ge(S["act_ok"], n - 1)
                pe.matmul(up_ps[n % 2][0:IW[j], :], w_gu[:, I + j * P:I + j * P + IW[j]],
                          onT[:, 2 * c + 1:2 * c + 3, 1, :], start=True, stop=True).then_inc(S["up_pe"], 1)

            def gate_up(n):
                gate(n)
                up(n)

            def down(n):
                c, j = divmod(n, NI)
                pe.wait_ge(S["act_ok"], n + 1)
                if n == 0:
                    pe.wait_ge(down_w_in, 16 * NI)
                    pe.wait_ge(S["o_ok"], NB)
                if n == NI:
                    pe.wait_ge(S["onT_ok"], NB + 1)
                if j == 0 and c >= 2:
                    pe.wait_ge(S["t1_ok"], c - 1)
                for t in range(TC):
                    ins = pe.matmul(down_ps[c % 2][:, t * P:(t + 1) * P], act_T[0:IW[j], n % 3, t * P:(t + 1) * P],
                                    w_down[0:IW[j], j, :], start=(j == 0 and t == 0), stop=(j == NI - 1),
                                    skip_group_check=True)
                ins.then_inc(S["down_pe"], 1)

            def turn_y(c):
                pe.wait_ge(S["y_ok"], c + 1)
                if c >= 1:
                    pe.wait_ge(S["ylo_ok"], c)
                if c == 0:
                    pe.wait_ge(S["bin2T_ok"], 1)
                for t in range(TC):
                    ins = pe.transpose(yT_ps[:, t * P:(t + 1) * P], y[:, c * TC + t, :], ident[:, :])
                ins.then_inc(S["yT_pe"], 1)

            def hidden(n):
                c, j = divmod(n, NF)
                if n >= 3:
                    pe.wait_ge(S["hid_ok"], n - 2)
                pe.wait_ge(S["yhi_ok"], c + 1)
                if n == 0:
                    pe.wait_ge(S["x2_ok"], NB)
                elif n < 3:
                    pe.wait_ge(S["gates_ok"], NC * NI - 2 + n)
                w = sign1T[:, j * P:(j + 1) * P]
                pe.matmul(hid_ps[n % 3][:, :], w, y_hi[:, c % 2, :], start=True, stop=False)
                pe.wait_ge(S["ylo_ok"], c + 1)
                pe.matmul(hid_ps[n % 3][:, :], w, y_lo[:, c % 2, :], start=False, stop=True).then_inc(S["hid_pe"], 1)

            def ffn_out(n):
                c, j = divmod(n, NF)
                pe.wait_ge(S["hid_ok"], n + 1)
                if j == 0 and c >= 2:
                    pe.wait_ge(S["t2_ok"], c - 1)
                elif j == 0:
                    pe.wait_ge(S["act_ok"], NC * NI - 1 + c)
                for t in range(TC):
                    ins = pe.matmul(ffn_ps(c, t), hid[:, n % 4, t * P:(t + 1) * P], bin2T[:, j, :],
                                    start=(j == 0 and t == 0), stop=(j == NF - 1), skip_group_check=True)
                ins.then_inc(S["ffn_pe"], 1)

            def ffn_out_last(t):
                if t == 0:
                    pe.wait_ge(S["t2_ok"], NC - 2)
                    pe.wait_ge(S["t1_ok"], NC)
                    pe.wait_ge(S["ylo_ok"], NC)
                for j in range(NF):
                    n = NF * (NC - 1) + j
                    pe.wait_ge(S["hid_ok"], n + 1)
                    ins = pe.matmul(ffn_ps(NC - 1, t), hid[:, n % 4, t * P:(t + 1) * P], bin2T[:, j, :],
                                    start=(j == 0), stop=(j == NF - 1))
                ins.then_inc(S["ffn_pe"], 1)

            def keep_busy(times):
                for _ in range(times):
                    pe.matmul(bank_o[:, 0:P], busy[:, :], busy[:, :], start=True, stop=True)

            pe.wait_ge(S["warm_ok"], 1)
            keep_busy(8)
            pe.wait_ge(S["ident_ok"], 1)
            pe.wait_ge(gk1_w_in, 16)
            pe.transpose(bank_uw[0:R, 0:P], gk1_in[:, :], ident[:, :]).then_inc(S["gk1T_ps"], 1)
            turn_x(0)
            keep_busy(1)
            pe.wait_ge(S["gk1T_ok"], 1)
            pe.wait_ge(gk2_w_in, 16)
            pe.matmul(bank_uw[:, 0:DK], gk1T[:, :], gk2_in[:, :], start=True, stop=True).then_inc(S["gkw_ps"], 1)
            keep_busy(1)
            project_qkz(0)
            turn_x(1)
            project_vg(0)
            keep_busy(3)
            pe.wait_ge(S["consts_ok"], 1)
            decay(0)
            project_vg(1)
            keep_busy(2)
            turn_qk(0)
            turn_x(2)
            project_qkz(1)
            for k in range(NB):
                scores(k)
                key_values(k)
                if k + 1 < NB:
                    decay(k + 1)
                outputs(k, 0)
                outputs(k, 1)
                if k >= 1:
                    turn_og_n(k - 1)
                if k == NB - 1:
                    up(0)
                if k + 2 < NB:
                    project_qkz(k + 2)
                if k + 1 < NB:
                    turn_qk(k + 1)
                if k + 3 < NB:
                    turn_x(k + 3)
                if k == NB - 1:
                    turn_bin2()
                if k == NB - 2:
                    turn_sign1()
                if k >= 1:
                    project_out(k - 1)
                if k == NB - 2:
                    gate(0)
                if k + 2 < NB:
                    project_vg(k + 2)
            gate_up(1)
            turn_og_n(NB - 1)
            gate_up(2)
            project_out(NB - 1)
            down(0)
            gate_up(3)
            down(1)
            turn_last_n()
            for n in range(4, NC * NI):
                down(n - 2)
                if n == 2 * NI + 1:
                    turn_y(0)
                if n == 3 * NI + 1:
                    turn_y(1)
                gate_up(n)
            down(NC * NI - 2)
            hidden(0)
            hidden(1)
            down(NC * NI - 1)
            for n in range(2, NF * (NC - 1) + 1):
                hidden(n)
                if n % NF == 3 and n // NF + 2 < NC:
                    turn_y(n // NF + 2)
                ffn_out(n - 2)
            for n in range(NF * (NC - 1) + 1, NF * NC - 1):
                hidden(n)
                if n < NF * (NC - 1) + 2:
                    ffn_out(n - 2)
            hidden(NF * NC - 1)
            for t in range(TC):
                ffn_out_last(t)

        @block.scalar
        def _(act):
            nc.scalar.preload_act_table_set("natural_log_exp_and_others")
            act.dma_start(anw[:, :], attn_norm_w.rearrange("(p a) -> p a", a=1)).then_inc(attn_w_in, 16)
            act.dma_start(w_in[:, 2 * DK:2 * DK + DV], Wv).then_inc(attn_w_in, 16)
            act.dma_start(w_in[:, 2 * DK + DV:2 * DK + VG], Wg).then_inc(attn_w_in, 16)

            def root(ssq_sem, ln_sem, rs_sem, value, ssq, ln, rs, width):
                act.wait_ge(S[ssq_sem], value)
                act.activation(ln, ssq, ACT.Ln, bias=eps[:, :], scale=1.0 / width).then_inc(S[ln_sem], 1)
                act.wait_ge(S[ln_sem], value)
                act.activation(rs, ln, ACT.Exp, scale=-0.5).then_inc(S[rs_sem], 1)

            def root_x(b):
                root("xssq_ok", "xln_ok", "xrs_ok", b + 1, x_ssq[:, tiles(b)], x_ln[:, tiles(b)],
                     x_rs[:, tiles(b)], D)

            def copy_xT(b):
                act.wait_ge(S["xT_pe"], b + 1)
                act.activation(xT[:, b * BT:(b + 1) * BT], xT_ps, ACT.Copy).then_inc(S["xT_ok"], 1)

            def copy_vg(b):
                act.wait_ge(S["vg_pe"], b + 1)
                act.activation(vg[:, tiles(b), :], vg_ps, ACT.Copy).then_inc(S["vg_ok"], 1)

            def soft_z(b):
                act.wait_ge(S["zna_ok"], b + 1)
                if b >= 1:
                    act.wait_ge(S["zl_ok"], b)
                act.activation(z_e[:, :, :], z_na[:, :, :], ACT.Exp).then_inc(S["ze_ok"], 1)
                act.wait_ge(S["ze_ok"], b + 1)
                if b >= 1:
                    act.wait_ge(S["glog_ok"], b)
                act.activation(z_l[:, :, :], z_e[:, :, :], ACT.Ln, bias=1.0).then_inc(S["zl_ok"], 1)

            def soft_g(b):
                act.wait_ge(S["gna_ok"], b + 1)
                act.activation(g_e[:, :, :], g_na[:, :, :], ACT.Exp).then_inc(S["ge_ok"], 1)
                act.wait_ge(S["ge_ok"], b + 1)
                if b >= 1:
                    act.wait_ge(S["gls_ok"], b)
                act.activation(g_l[:, :, :], g_e[:, :, :], ACT.Ln, bias=1.0).then_inc(S["gl_ok"], 1)

            def sigmoid_g(b):
                act.wait_ge(S["gls_ok"], b + 1)
                if b >= 1:
                    act.wait_ge(S["gs_ok"], b)
                act.activation(g_sg[:, :, :], g_ls[:, :, :], ACT.Exp).then_inc(S["gsg_ok"], 1)

            def decays(b):
                act.wait_ge(S["carry_pe"], b + 1)
                if b >= 1:
                    act.wait_ge(S["qe_ok"], b)
                act.activation(grow[:, :], decay_ps, ACT.Exp).then_inc(S["grow_ok"], 1)
                if b >= 1:
                    act.wait_ge(S["ke_ok"], b)
                act.activation(fall[:, :], decay_ps, ACT.Exp, scale=-1.0).then_inc(S["fall_ok"], 1)
                if b >= 2:
                    act.wait_ge(S["kv_ok"], b - 1)
                act.activation(carry[:, b % 2, :], carry_ps, ACT.Exp).then_inc(S["carry_ok"], 1)

            def copy_qk(b):
                act.wait_ge(S["turn_pe"], b + 1)
                if b == 0:
                    act.wait_ge(S["pads_ok"], 1)
                if b >= 2:
                    act.wait_ge(S["a_pe"], TB * (b - 1))
                    act.wait_ge(S["o_pe"], b - 1)
                act.activation(kT[:, b % 2, :], bank_turn[:, 0:BT], ACT.Copy).then_inc(S["kT_ok"], 1)
                for t in range(TB):
                    for h in range(H):
                        rows = slice(h * HP, (h + 1) * HP)
                        ins = act.activation(qheads[rows, b % 2, t, h, :],
                                             bank_turn[rows, BT + t * P:BT + (t + 1) * P], ACT.Copy)
                    ins.then_inc(S["qheads_ok"], 1)
                act.activation(qT1[:, b % 2, :], bank_turn[:, BT + P:2 * BT], ACT.Copy).then_inc(S["qT1_ok"], 1)

            def copy_o(b):
                act.wait_ge(S["o_pe"], b + 1)
                if b >= 2:
                    act.wait_ge(S["on_ok"], b - 1)
                    act.wait_ge(S["osq_ok"], b - 1)
                act.activation(o_sb[:, b % 2], o_ps, ACT.Copy).then_inc(S["o_ok"], 1)

            def root_o(b):
                root("ossq_ok", "oln_ok", "ors_ok", b + 1, o_ssq[:, tiles(b), :], o_ln[:, tiles(b), :],
                     o_rs[:, tiles(b), :], E)

            def copy_on(s):
                act.wait_ge(S["ogT_pe"], s + 1)
                a, z = 0, (2 if 1 <= s < NB - 1 else 1)
                act.activation(onT[:, s, a:z, :], bank_vg[:, a * BT:z * BT].rearrange("p (a c) -> p a c", c=BT),
                               ACT.Copy).then_inc(S["onT_ok"], 1)

            def copy_last_n():
                act.wait_ge(S["ogT_pe"], NB + 1)
                act.activation(onT[:, NB - 1:NB + 1, 1, :], bank_vg[:, :].rearrange("p (a c) -> p a c", c=BT),
                               ACT.Copy).then_inc(S["onT_ok"], 1)

            def silu(n):
                j = n % NI
                act.wait_ge(S["gate_pe"], n + 1)
                if n >= 2:
                    act.wait_ge(S["act_ok"], n - 1)
                act.activation(gate_s[0:IW[j], n % 2, :], gate_ps[n % 2][0:IW[j], :], ACT.Silu)\
                    .then_inc(S["gates_ok"], 1)

            def copy_sign1T():
                act.wait_ge(S["sign1T_ps"], 1)
                act.activation(sign1T[:, :], signs_ps[:, :], ACT.Copy).then_inc(S["sign1T_ok"], 1)

            def copy_bin2T():
                act.wait_ge(S["bin2T_ps"], 1)
                act.activation(bin2T[:, :, :], signs_ps[:, :].rearrange("p (j d) -> p j d", j=NF), ACT.Copy)\
                    .then_inc(S["bin2T_ok"], 1)

            def high_y(c):
                act.wait_ge(S["yT_pe"], c + 1)
                if c >= 2:
                    act.wait_ge(S["hid_pe"], NF * (c - 1))
                act.activation(y_hi[:, c % 2, :], yT_ps[:, :], ACT.Copy).then_inc(S["yhi_ok"], 1)

            def gelu(n):
                c, j = divmod(n, NF)
                act.wait_ge(S["hid_pe"], n + 1)
                if n >= 4:
                    act.wait_ge(S["ffn_pe"], n - 3)
                act.activation(hid[:, n % 4, :], hid_ps[n % 3][:, :], ACT.Gelu, bias=b1_col[:, j:j + 1],
                               scale=alpha1[:, j:j + 1]).then_inc(S["hid_ok"], 1)

            def normalize2(c):
                act.wait_ge(S["nb_ok"], 1)
                for t in range(TC):
                    ins = act.activation(y_out[:, c * TC + t, :], ln_in[:, c % 2, t, :], ACT.Identity,
                                         bias=ln_nb[:, t:t + 1], scale=ln_rs[:, c % 2, t:t + 1])
                ins.then_inc(S["yout_act"], 1)

            act.wait_ge(S["eps_ok"], 1)
            root_x(0)
            copy_xT(0)
            act.wait_ge(attn_w_in, 80)
            act.activation(w_vg[:, :], w_in[:, 2 * DK:2 * DK + VG], ACT.Copy, scale=anw[:, 0:1])\
                .then_inc(S["w_vg_ok"], 1)
            root_x(1)
            copy_xT(1)
            soft_z(0)
            copy_vg(0)
            decays(0)
            root_x(2)
            soft_g(0)
            root_x(3)
            copy_qk(0)
            soft_z(1)
            sigmoid_g(0)
            copy_xT(2)
            copy_vg(1)
            for k in range(NB):
                if k >= 1:
                    root_o(k - 1)
                if k + 4 < NB:
                    root_x(k + 4)
                if k + 1 < NB:
                    decays(k + 1)
                    soft_g(k + 1)
                copy_o(k)
                if k >= 1:
                    copy_on(k - 1)
                if k == NB - 1:
                    root_o(NB - 1)
                if k + 1 < NB:
                    copy_qk(k + 1)
                if k + 2 < NB:
                    soft_z(k + 2)
                if k + 1 < NB:
                    sigmoid_g(k + 1)
                if k + 3 < NB:
                    copy_xT(k + 3)
                if k + 2 < NB:
                    copy_vg(k + 2)
                if k == NB - 2:
                    copy_sign1T()
            nc.scalar.preload_act_table_set("silu_and_others")
            silu(0)
            copy_bin2T()
            silu(1)
            copy_on(NB - 1)
            silu(2)
            silu(3)
            copy_last_n()
            for n in range(4, NC * NI):
                silu(n)
                if n == 2 * NI + 1:
                    high_y(0)
                if n == 3 * NI + 1:
                    high_y(1)
            nc.scalar.preload_act_table_set("gelu_and_others")
            act.wait_ge(S["alpha_ok"], 2)
            for n in range(NC * NF):
                gelu(n)
                if n % NF == 3 and n // NF + 2 < NC:
                    high_y(n // NF + 2)
            normalize2(NC - 2)

        @block.vector
        def _(dve):
            dve.memset(busy[:, :], 0.0).then_inc(S["warm_ok"], 1)
            dve.memset(eps[:, :], RMS_EPS).then_inc(S["eps_ok"], 1)
            half = P // 2
            dve.memset(late_half[0:half, :], 0.0)
            dve.memset(late_half[half:P, :], 1.0 / GATE_NORMALIZER)
            dve.memset(early_half[0:half, :], 1.0 / GATE_NORMALIZER)
            dve.memset(early_half[half:P, :], 0.0)
            dve.memset(same_head[:, :], 0.0).then_inc(S["same_zero"], 1)
            dve.wait_ge(S["same_zero"], 1)
            for h in range(H):
                dve.memset(same_head[h * HP:(h + 1) * HP, h * E:(h + 1) * E], 1.0)

            def squares_x(b):
                dve.wait_ge(x_in[b], 16)
                for t in range(TB):
                    i = b * TB + t
                    ins = dve.tensor_tensor_reduce(xh[:, i, :], xs[:, i, :], xs[:, i, :], 1.0, 0.0, ALU.mult,
                                                   ALU.add, x_ssq[:, i:i + 1])
                ins.then_inc(S["xssq_ok"], 1)

            def scale_x(b):
                dve.wait_ge(S["xrs_ok"], b + 1)
                for t in range(TB):
                    i = b * TB + t
                    ins = dve.tensor_scalar(xh[:, i, :], xs[:, i, :], x_rs[:, i:i + 1], None, ALU.mult)
                ins.then_inc(S["xh_ok"], 1)

            def z_start(b):
                dve.wait_ge(S["qkz_pe"], b + 1)
                bias = z_bias[:, :].unsqueeze(1).to_broadcast([P, TB, DK])
                if b >= 1:
                    dve.wait_ge(S["glog_ok"], b)
                dve.tensor_tensor(zb[:, :, :], qkz_ps[:, :, 2 * DK:QKZ], bias, ALU.add).then_inc(S["zb_ok"], 1)
                dve.wait_ge(S["zb_ok"], b + 1)
                if b >= 1:
                    dve.wait_ge(S["ze_ok"], b)
                dve.scalar_tensor_tensor(out=z_na[:, :, :], in0=zb[:, :, :], scalar=-1.0, in1=zb[:, :, :],
                                         op0=ALU.mult, op1=ALU.min).then_inc(S["zna_ok"], 1)

            def z_end(b):
                dve.wait_ge(S["zl_ok"], b + 1)
                if b == 0:
                    dve.wait_ge(S["pads_ok"], 1)
                if b >= 2:
                    dve.wait_ge(S["carry_pe"], b - 1)
                g4 = glog[:, b % 2].rearrange("p t (h d) -> p (t h) d", d=HP)[:, :, 0:HD]
                dve.scalar_tensor_tensor(out=g4, in0=zb[:, :, :].rearrange("p t (h d) -> p (t h) d", d=HD),
                                         scalar=0.0, in1=z_l[:, :, :].rearrange("p t (h d) -> p (t h) d", d=HD),
                                         op0=ALU.min, op1=ALU.subtract).then_inc(S["glog_ok"], 1)

            def g_start(b):
                dve.wait_ge(S["vg_ok"], b + 1)
                if b >= 1:
                    dve.wait_ge(S["ge_ok"], b)
                dve.scalar_tensor_tensor(out=g_na[:, :, :], in0=vg[:, tiles(b), DV:VG], scalar=-1.0,
                                         in1=vg[:, tiles(b), DV:VG], op0=ALU.mult, op1=ALU.min)\
                    .then_inc(S["gna_ok"], 1)

            def g_end(b):
                dve.wait_ge(S["gl_ok"], b + 1)
                if b >= 1:
                    dve.wait_ge(S["gsg_ok"], b)
                dve.scalar_tensor_tensor(out=g_ls[:, :, :], in0=vg[:, tiles(b), DV:VG], scalar=0.0,
                                         in1=g_l[:, :, :], op0=ALU.min, op1=ALU.subtract).then_inc(S["gls_ok"], 1)

            def scale_qk(b):
                if b >= 2:
                    dve.wait_ge(S["turn_pe"], b - 1)
                    dve.wait_ge(S["kv_pe"], b - 1)

                def heads(ap, width):
                    return ap.rearrange("p t (h d) -> p t h d", d=width)[:, :, :, 0:HD]
                dve.wait_ge(S["grow_ok"], b + 1)
                q_in = heads(qkz_ps[:, :, 0:DK], HD)
                k_in = heads(qkz_ps[:, :, DK:2 * DK], HD)
                g_in = grow[:, :].rearrange("p (t h d) -> p t h d", t=TB, h=H)
                f_in = fall[:, :].rearrange("p (t h d) -> p t h d", t=TB, h=H)
                dve.wait_ge(S["fall_ok"], b + 1)
                dve.tensor_tensor(heads(qe[:, b % 2], HP), q_in, g_in, ALU.mult).then_inc(S["qe_ok"], 1)
                dve.tensor_tensor(heads(ke[:, b % 2], HP), k_in, f_in, ALU.mult).then_inc(S["ke_ok"], 1)

            def mask(b, t):
                dve.wait_ge(S["a_pe"], TB * b + t + 1)
                if b == 0:
                    dve.wait_ge(S["pads_ok"], 2)
                if b >= 2:
                    dve.wait_ge(S["o_pe"], b - 1)
                dve.copy_predicated(att[:, b % 2, t, :], causal[:, :].bitcast(U32), bank_a[t][:, :])\
                    .then_inc(S["att_ok"], 1)

            def make_state(b):
                dve.wait_ge(S["kv_pe"], b + 1)
                dve.wait_ge(S["carry_ok"], b + 1)
                if b == 0:
                    dve.wait_ge(S["consts_ok"], 1)
                if b >= 2:
                    dve.wait_ge(S["o_pe"], b - 1)
                dve.scalar_tensor_tensor(out=state[:, b % 2, :], in0=kv_ps, scalar=carry[:, b % 2, 0:1],
                                         in1=same_head[:, :], op0=ALU.mult, op1=ALU.mult)\
                    .then_inc(S["kv_ok"], 1)

            def norm_o(b):
                dve.wait_ge(S["osq_ok"], b + 1)
                dve.tensor_reduce(o_ssq[:, tiles(b), :], o_sq[:, b % 2].rearrange("p t (h e) -> p t h e", e=E),
                                  AX.X, ALU.add).then_inc(S["ossq_ok"], 1)

            def gated(b):
                dve.wait_ge(S["ors_ok"], b + 1)
                rs = o_rs[:, tiles(b), :].unsqueeze(3).to_broadcast([P, TB, H, E])
                if b >= 1:
                    dve.wait_ge(S["og_ok"], b)
                dve.tensor_tensor(o_n[:, :, :].rearrange("p t (h e) -> p t h e", e=E),
                                  o_sb[:, b % 2].rearrange("p t (h e) -> p t h e", e=E), rs, ALU.mult)\
                    .then_inc(S["on_ok"], 1)
                dve.wait_ge(S["on_ok"], b + 1)
                dve.wait_ge(S["gs_ok"], b + 1)
                if b >= 2:
                    dve.wait_ge(S["ogT_pe"], b - 1)
                dve.tensor_tensor(og[:, b % 2], o_n[:, :, :], gs[:, b % 2], ALU.mult).then_inc(S["og_ok"], 1)

            def residual(b):
                dve.wait_ge(S["wo_pe"], b + 1)
                dve.tensor_tensor(x2[:, tiles(b), :], wo_ps, xs[:, tiles(b), :], ALU.add).then_inc(S["x2_ok"], 1)
                dve.wait_ge(S["x2_ok"], b + 1)
                for t in range(TB):
                    i = b * TB + t
                    ins = dve.tensor_tensor_reduce(y[:, i, :], x2[:, i, :], x2[:, i, :], 1.0, 0.0, ALU.mult,
                                                   ALU.add, x2_ssq[:, i:i + 1])
                ins.then_inc(S["x2ssq_ok"], 1)

            def scale_x2(b):
                dve.wait_ge(S["x2rs_ok"], b + 1)
                if b >= 2:
                    dve.wait_ge(S["ogT_pe"], b)
                for t in range(TB):
                    i = b * TB + t
                    ins = dve.tensor_scalar(n_sb[:, b % 2, t, :], x2[:, i, :], x2_rs[:, i:i + 1], None, ALU.mult)
                ins.then_inc(S["n_ok"], 1)

            squares_x(0)
            scale_x(0)
            dve.wait_ge(S["gk1T_ps"], 1)
            dve.tensor_copy(gk1T[:, :], bank_uw[0:R, 0:P]).then_inc(S["gk1T_ok"], 1)
            dve.wait_ge(attn_w_in, 80)
            dve.tensor_scalar(w_qkz[:, 0:DK], w_in[:, 0:DK], anw[:, 0:1], float(HD) ** -0.5, ALU.mult, ALU.mult)
            dve.tensor_scalar(w_qkz[:, DK:2 * DK], w_in[:, DK:2 * DK], anw[:, 0:1], None, ALU.mult)\
                .then_inc(S["w_qkz_ok"], 1)
            squares_x(1)
            dve.wait_ge(S["gkw_ps"], 1)
            dve.tensor_scalar(w_qkz[:, 2 * DK:QKZ], bank_uw[:, 0:DK], anw[:, 0:1], None, ALU.mult)\
                .then_inc(S["w_qkz_ok"], 1)
            scale_x(1)
            squares_x(2)
            dve.wait_ge(S["up_to_ok"], 1)
            dve.tensor_scalar(decay_sum[0:half, :], decay_sum[0:half, :], -1.0 / GATE_NORMALIZER, None, ALU.add)\
                .then_inc(S["consts_ok"], 1)

            def prepare_o():
                dve.wait_ge(wo_w_in, 16 * (1 + H))
                dve.tensor_scalar(w_o[:, :], wo_in[:, :], gnw[:, 0:1], None, ALU.mult).then_inc(S["w_o_ok"], 1)

            def prepare_mlp():
                dve.wait_ge(mlp_w_in, 48)
                dve.tensor_scalar(w_gu[:, :], gu_in[:, :], mnw[:, 0:1], None, ALU.mult).then_inc(S["w_gu_ok"], 1)

            def magnitude1():
                dve.wait_ge(ffn_w_in, 64)
                dve.tensor_reduce(abs1[:, :], w1_in[:, :, :], AX.X, ALU.add, apply_absolute_value=True)\
                    .then_inc(S["abs_ok"], 1)

            def magnitude2():
                dve.tensor_reduce(abs2[:, :], w2_in[:, :], AX.X, ALU.add, apply_absolute_value=True)\
                    .then_inc(S["abs_ok"], 1)

            def scale_sign2():
                dve.wait_ge(S["abs_ok"], 2)
                dve.tensor_scalar(alpha2[:, :], abs2[:, :], 1.0 / HF, None, ALU.mult).then_inc(S["alpha_ok"], 1)
                dve.tensor_scalar(alpha1[:, :], abs1[:, :], 1.0 / D, None, ALU.mult).then_inc(S["alpha_ok"], 1)
                dve.wait_ge(S["alpha_ok"], 2)
                dve.wait_ge(S["sign2_ok"], 1)
                dve.tensor_scalar(bin2[:, :], sign2[:, :], alpha2[:, 0:1], None, ALU.mult).then_inc(S["bin2_ok"], 1)

            dve.wait_ge(z_bias_in, 16)
            z_start(0)
            z_end(0)
            g_start(0)
            squares_x(3)
            scale_qk(0)
            scale_x(2)
            g_end(0)
            squares_x(4)
            scale_x(3)
            prepare_o()
            z_start(1)
            for k in range(NB):
                if k + 1 < NB:
                    z_end(k + 1)
                mask(k, 0)
                if k >= 2:
                    scale_x2(k - 2)
                if k + 1 < NB:
                    g_start(k + 1)
                mask(k, 1)
                make_state(k)
                if k >= 1:
                    gated(k - 1)
                if k + 1 < NB:
                    scale_qk(k + 1)
                    g_end(k + 1)
                if k + 4 < NB:
                    scale_x(k + 4)
                if k + 5 < NB:
                    squares_x(k + 5)
                if k == 0:
                    prepare_mlp()
                if k == NB - 4:
                    magnitude1()
                if k == NB - 3:
                    magnitude2()
                if k == NB - 1:
                    scale_sign2()
                norm_o(k)
                if k == NB - 1:
                    gated(k)
                if k + 2 < NB:
                    z_start(k + 2)
                if k >= 1:
                    residual(k - 1)

            def gated_up(n):
                j = n % NI
                dve.wait_ge(S["up_pe"], n + 1)
                dve.wait_ge(S["gates_ok"], n + 1)
                if n >= 3:
                    dve.wait_ge(S["down_pe"], n - 2)
                dve.tensor_tensor(act_T[0:IW[j], n % 3, :], up_ps[n % 2][0:IW[j], :], gate_s[0:IW[j], n % 2, :],
                                  ALU.mult).then_inc(S["act_ok"], 1)

            def moments(c, a, z, which, g, source, addend, between=None):
                q = c % 2
                dve.tensor_tensor(ln_in[:, q, a:z], source.rearrange("p (t d) -> p t d", d=D),
                                  addend[:, c * TC + a:c * TC + z, :], ALU.add).then_inc(S["t" + which], 1)
                if between is not None:
                    normalize2(between)
                dve.wait_ge(S["t" + which], g + 1)
                for t in range(a, z):
                    ins = dve.bn_stats(ln_st[:, q, t, :], ln_in[:, q, t, :])
                ins.then_inc(S["st" + which], 1)
                dve.wait_ge(S["st" + which], g + 1)
                for t in range(a, z):
                    ins = dve.bn_aggr(ln_mv[:, q, t, :], ln_st[:, q, t, :])
                ins.then_inc(S["mv" + which], 1)

            def moments1(c):
                dve.wait_ge(S["xx2_ok"], (c + 1) * TC // TB)
                dve.wait_ge(S["down_pe"], NI * (c + 1))
                moments(c, 0, TC, "1_ok", c, down_ps[c % 2][:, :], xx2)

            def normalize(c, a, z, which, g, dest, done):
                dve.wait_ge(S["rs" + which], g + 1)
                for t in range(a, z):
                    ins = dve.tensor_scalar(dest[:, c * TC + t, :], ln_in[:, c % 2, t, :], ln_mv[:, c % 2, t, 0:1],
                                            ln_rs[:, c % 2, t:t + 1], ALU.subtract, ALU.mult)
                ins.then_inc(S[done], 1)

            def normalize1(c):
                normalize(c, 0, TC, "1_ok", c, y, "y_ok")

            def low_y(c):
                dve.wait_ge(S["yhi_ok"], c + 1)
                if c >= 2:
                    dve.wait_ge(S["hid_pe"], NF * (c - 1))
                dve.tensor_tensor(y_lo[:, c % 2, :], yT_ps[:, :], y_hi[:, c % 2, :].bitcast(F32), ALU.subtract)\
                    .then_inc(S["ylo_ok"], 1)

            def moments2(g, between=None):
                c, a, z = steps2[g]
                dve.wait_ge(S["yb_ok"], c + 1)
                dve.wait_ge(S["ffn_pe"], NF * (c + 1) if c < NC - 1 else NF * (NC - 1) + z)
                moments(c, a, z, "2_ok", g, ffn_ps(c, a) if z == a + 1 else bank_a[c % 2][:, :], yb, between)

            def normalize2(g):
                c, a, z = steps2[g]
                normalize(c, a, z, "2_ok", g, y_out, "yout_ok")

            gated_up(0)
            scale_x2(NB - 2)
            gated_up(1)
            residual(NB - 1)
            gated_up(2)
            scale_x2(NB - 1)
            for n in range(3, NC * NI):
                gated_up(n)
                if n % NI == 1:
                    moments1(n // NI - 1)
                if n == 2 * NI + 1:
                    low_y(0)
                if n == 3 * NI + 1:
                    low_y(1)
                if n % NI == 2:
                    normalize1(n // NI - 1)
            moments1(NC - 1)
            normalize1(NC - 1)
            for g in range(len(steps2)):
                if g + 2 < NC:
                    low_y(g + 2)
                moments2(g, between=g - 2 if g > NC else None)
                if g < NC - 2:
                    normalize2(g)
            normalize2(len(steps2) - 2)
            normalize2(len(steps2) - 1)


_INS = ['L0_attn_hidden_states', 'L0_attn_attn_norm_w', 'L0_attn_Wq', 'L0_attn_Wk', 'L0_attn_Wv', 'L0_attn_Wg',
        'L0_attn_Wgk1', 'L0_attn_Wgk2', 'L0_attn_bgk2', 'L0_attn_gnorm_w', 'L0_attn_Wo', 'L0_attn_mlp_norm_w',
        'L0_attn_W_gate', 'L0_attn_W_up', 'L0_attn_W_down', 'L0_ffn_w1', 'L0_ffn_b1', 'L0_ffn_w2', 'L0_ffn_b2']


def kernel(**inputs):
    import numpy as np
    import concourse.bacc as bacc
    from concourse.bass_utils import run_bass_kernel_spmd

    nc = bacc.Bacc("TRN2", target_bir_lowering=False, num_devices=1)
    arrays, args = {}, []
    for name in _INS:
        a = np.ascontiguousarray(inputs[name])
        arrays[f"in_{name}_dram"] = a
        args.append(nc.dram_tensor(f"in_{name}_dram", a.shape, mybir.dt.from_np(a.dtype), kind="ExternalInput").ap())
    shape = inputs['L0_attn_hidden_states'].shape
    args.append(nc.dram_tensor("out_dram", shape, F32, kind="ExternalOutput").ap())
    gla_block_and_binary_ffn(nc, *args)
    result = run_bass_kernel_spmd(nc, [arrays], core_ids=[0])
    return result.results[0]["out_dram"]
```
